# Optimizing a Trainium2 kernel written in Bass

```python
import numpy as np
import jax
import jax.numpy as jnp

def _softmax(x, axis=-1):
    return jax.nn.softmax(x, axis=axis)
def _gelu(x):
    return jax.nn.gelu(x, approximate=True)
def _silu(x):
    return jax.nn.silu(x)
def _sigmoid(x):
    return jax.nn.sigmoid(x)
def _layernorm(x, axis=-1, eps=1e-5):
    m = jnp.mean(x, axis=axis, keepdims=True)
    v = jnp.var(x, axis=axis, keepdims=True)
    return (x - m) / jnp.sqrt(v + eps)
def _scatter_add(tgt, idx, src, axis=0):
    return tgt.at[idx].add(src)
def _segment_sum(src, seg, n):
    return jax.ops.segment_sum(src, seg, n)

kernel_name = 'mk_conv_preact_d1_conv_nchw512_f99206'

def setup_inputs(seed: int = 0):
    np.random.seed(seed)
    _w = jnp.asarray
    def _rec_inputs():
        import jax
        import jax.numpy as jnp
        _gk = jax.random.key(seed)
        x = -8.268e-05 + 0.9999 * jax.random.normal(jax.random.fold_in(_gk, 1), (32, 512, 56, 56), jnp.float32)
        return x
    x = _rec_inputs()
    def _L0_conv_setup():
        import jax, jax.numpy as jnp
        import numpy as np
        N, C, H, W = (32, 512, 56, 56)
        M = 4
        CM = C // M
        K1 = 5
        K2 = 3
        P2 = 512 // 2

        def _dw_conv(f, kern, dil, pad):
            n, cm, h, w = f.shape
            fr = f.reshape(1, n * cm, h, w)
            kr = kern.reshape(n * cm, 1, kern.shape[-2], kern.shape[-1])
            o = jax.lax.conv_general_dilated(fr, kr, window_strides=(1, 1), padding=[(pad, pad), (pad, pad)], rhs_dilation=(dil, dil), feature_group_count=n * cm, dimension_numbers=('NCHW', 'OIHW', 'NCHW'))
            return o.reshape(n, cm, h, w)
        key = jax.random.key(seed)
        ks = jax.random.split(key, 13)
        s = lambda i, shape: jax.random.normal(ks[i], shape, jnp.float32) * 0.05
        return dict(x=jax.random.normal(ks[0], (N, C, H, W), jnp.float32), W_conv=s(1, (CM, C)), b_conv=s(2, (CM,)), wk=s(3, (K1 * K1,)), bk=s(4, (K1 * K1,)), wck=s(5, ()), bck=s(6, ()), wk2=s(7, (K2 * K2,)), bk2=s(8, (K2 * K2,)), wck2=s(9, ()), bck2=s(10, ()), W_fuse=s(11, (P2, CM)), b_fuse=s(12, (P2,)))
    _L0_conv_all = _L0_conv_setup()
    _L0_conv_in = {k: v for k, v in _L0_conv_all.items() if k in ('W_conv', 'b_conv', 'wk', 'bk', 'wck', 'bck', 'wk2', 'bk2', 'wck2', 'bck2', 'W_fuse', 'b_fuse', )}
    del _L0_conv_all

    return {
        "x": x,
        "L0_conv_W_conv": _L0_conv_in["W_conv"],
        "L0_conv_b_conv": _L0_conv_in["b_conv"],
        "L0_conv_wk": _L0_conv_in["wk"],
        "L0_conv_bk": _L0_conv_in["bk"],
        "L0_conv_wck": _L0_conv_in["wck"],
        "L0_conv_bck": _L0_conv_in["bck"],
        "L0_conv_wk2": _L0_conv_in["wk2"],
        "L0_conv_bk2": _L0_conv_in["bk2"],
        "L0_conv_wck2": _L0_conv_in["wck2"],
        "L0_conv_bck2": _L0_conv_in["bck2"],
        "L0_conv_W_fuse": _L0_conv_in["W_fuse"],
        "L0_conv_b_fuse": _L0_conv_in["b_fuse"],
    }

def reference(x, L0_conv_W_conv, L0_conv_b_conv, L0_conv_wk, L0_conv_bk, L0_conv_wck, L0_conv_bck, L0_conv_wk2, L0_conv_bk2, L0_conv_wck2, L0_conv_bck2, L0_conv_W_fuse, L0_conv_b_fuse):
    import jax
    import jax.numpy as jnp
    def _L0_conv_ref(x, W_conv, b_conv, wk, bk, wck, bck, wk2, bk2, wck2, bck2, W_fuse, b_fuse):
        import jax, jax.numpy as jnp
        import numpy as np
        N, C, H, W = (32, 512, 56, 56)
        M = 4
        CM = C // M
        K1 = 5
        K2 = 3
        P2 = 512 // 2

        def _dw_conv(f, kern, dil, pad):
            n, cm, h, w = f.shape
            fr = f.reshape(1, n * cm, h, w)
            kr = kern.reshape(n * cm, 1, kern.shape[-2], kern.shape[-1])
            o = jax.lax.conv_general_dilated(fr, kr, window_strides=(1, 1), padding=[(pad, pad), (pad, pad)], rhs_dilation=(dil, dil), feature_group_count=n * cm, dimension_numbers=('NCHW', 'OIHW', 'NCHW'))
            return o.reshape(n, cm, h, w)
        f = jax.nn.relu(jnp.einsum('nchw,oc->nohw', x, W_conv) + b_conv[None, :, None, None])
        g = jax.nn.relu(x.mean((2, 3)) @ W_conv.T + b_conv)
        kern1 = ((g[:, :, None] * wk + bk) * wck + bck).reshape(N, CM, K1, K1)
        kern2 = ((g[:, :, None] * wk2 + bk2) * wck2 + bck2).reshape(N, CM, K2, K2)
        o1 = _dw_conv(f, kern1, dil=1, pad=(K1 - 1) // 2)
        o2 = _dw_conv(f, kern2, dil=2, pad=2)
        y1 = jnp.einsum('nchw,oc->nohw', o1, W_fuse) + b_fuse[None, :, None, None]
        y2 = jnp.einsum('nchw,oc->nohw', o2, W_fuse) + b_fuse[None, :, None, None]
        return jnp.concatenate([y1, y2], axis=1)

    def _gn(v, G=32, eps=1e-5):
        B_, C_, H_, W_ = v.shape
        g = v.reshape(B_, G, C_ // G, H_, W_)
        m = jnp.mean(g, axis=(2, 3, 4), keepdims=True)
        s = jnp.var(g, axis=(2, 3, 4), keepdims=True)
        return ((g - m) / jnp.sqrt(s + eps)).reshape(v.shape)

    def _ln_c(v, eps=1e-6):
        m = jnp.mean(v, axis=1, keepdims=True)
        s = jnp.var(v, axis=1, keepdims=True)
        return (v - m) / jnp.sqrt(s + eps)

    def _ln_t(v, eps=1e-5):
        m = jnp.mean(v, axis=-1, keepdims=True)
        s = jnp.var(v, axis=-1, keepdims=True)
        return (v - m) / jnp.sqrt(s + eps)

    def _to_tokens(v):
        B_, C_, H_, W_ = v.shape
        return v.reshape(B_, C_, H_ * W_).transpose(0, 2, 1)
    def _from_tokens(t, like):
        B_, C_, H_, W_ = like.shape
        return t.transpose(0, 2, 1).reshape(B_, C_, H_, W_)

    x = x + _L0_conv_ref(_gn(x), L0_conv_W_conv, L0_conv_b_conv, L0_conv_wk, L0_conv_bk, L0_conv_wck, L0_conv_bck, L0_conv_wk2, L0_conv_bk2, L0_conv_wck2, L0_conv_bck2, L0_conv_W_fuse, L0_conv_b_fuse)
    return x


_drawn_inputs = setup_inputs


def setup_inputs(seed=0):
    import zlib

    import numpy as np

    out = dict(_drawn_inputs(seed))
    spreads = {}
    factors = {'L0_conv_b_conv': 3.98,
     'L0_conv_wk': 64.0,
     'L0_conv_bk': 39.633,
     'L0_conv_wk2': 200.0,
     'L0_conv_bk2': 200.0}
    for name, (base, spread) in spreads.items():
        noise = np.random.default_rng([zlib.crc32(name.encode()), seed]).standard_normal(out[name].shape)
        drawn = base * np.exp(spread * noise) if base else spread * noise
        out[name] = jnp.asarray(drawn.astype(out[name].dtype))
    for name, factor in factors.items():
        out[name] = (out[name] * factor).astype(out[name].dtype)
    return out
```

```python
from contextlib import ExitStack

import concourse.bass as bass
from concourse import mybir

ALU = mybir.AluOpType
ACT = mybir.ActivationFunctionType
F32 = mybir.dt.float32
F32R = mybir.dt.float32r

P = 128
N, C, H, W = 32, 512, 56, 56
CM = 128
CT = C // P
CPG = 16
EPS = 1e-5
K1, K2 = 5, 3
HALO = 2
HW = H * W

GROUP_ROWS = 8
GROUPS = H // GROUP_ROWS
CHUNK = GROUP_ROWS * W
BAND_ROWS = GROUP_ROWS // 2
BAND = BAND_ROWS * W
TILE_COLS = 14
TILES = W // TILE_COLS
TILE = GROUP_ROWS * TILE_COLS
WIN_ROWS = GROUP_ROWS + 2 * HALO
WIN_COLS = TILE_COLS + 2 * HALO
WIN = WIN_ROWS * WIN_COLS

RING = 2 * GROUPS
AHEAD = RING - 1
CHUNKS = N * GROUPS

BN = 6
Y_STEP = CT
Y_IMAGE = Y_STEP * (GROUPS + 1)
Y_BANKS = 2
O_IMAGE = 2 * GROUPS
VAR_AT, PAIR_AT = 2 * CT, 16
NORM_STEPS = 11
ODD, EVEN, TAIL = range(3)


def window(q):
    left, right = TILE_COLS * q - HALO, TILE_COLS * (q + 1) + HALO
    lo, hi = max(left, 0), min(right, W)
    return lo, hi, lo - left, hi - left


def build(nc, x, w_conv, b_conv, wk, bk, wck, bck, wk2, bk2, wck2, bck2, w_fuse, b_fuse, out):
    x_chunks = x.rearrange("n (t p) h w -> n p t (h w)", p=P)
    out_chunks = out.rearrange("n (t p) h w -> n p t (h w)", p=P)

    with ExitStack() as ctx:
        def sb(name, shape, dt=F32):
            return ctx.enter_context(nc.sbuf_tensor(name, shape, dt))

        def bank(name):
            return ctx.enter_context(nc.psum_tensor(name, [P, 512], F32))

        def sem(name):
            return ctx.enter_context(nc.semaphore(name))

        x_ring = sb("x_ring", [P, CT, RING * CHUNK])
        x_hi = sb("x_hi", [P, CT, CHUNK], F32R)
        x_lo = sb("x_lo", [P, CT, CHUNK], F32R)
        f_row = sb("f_row", [P, 2, TILES, TILE])
        ft_hi = sb("ft_hi", [P, 2, 2, TILES * CM], F32R)
        ft_lo = sb("ft_lo", [P, 2, 2, TILES * CM], F32R)
        o_hi = sb("o_hi", [P, 3, 2, BAND], F32R)
        o_lo = sb("o_lo", [P, 3, 2, BAND], F32R)
        band_hi = sb("band_hi", [P, 2, 2, WIN], F32R)
        band_lo = sb("band_lo", [P, 2, 2, WIN], F32R)
        band_f32 = sb("band_f32", [P, 2, 2, WIN])
        shifts = sb("shifts", [P, WIN_ROWS + 2 * HALO, WIN_COLS + 2 * HALO])
        wconv_raw = sb("wconv_raw", [P, C])
        wfuse_raw = sb("wfuse_raw", [P, 2, CM])
        wconv_t = sb("wconv_t", [P, CT, CM])
        wn = sb("wn", [P, CT, CM])
        wn_hi = sb("wn_hi", [P, CT, CM], F32R)
        wn_lo = sb("wn_lo", [P, CT, CM], F32R)
        wfuse_t = sb("wfuse_t", [P, 2, P])
        wfuse_hi = sb("wfuse_hi", [P, 2, P], F32R)
        wfuse_lo = sb("wfuse_lo", [P, 2, P], F32R)
        ident = sb("ident", [P, P])
        group_avg = sb("group_avg", [P, P])
        ones = sb("ones", [1, P])
        T1, T2 = K1 * K1, K2 * K2
        KC = 2 * T1 + 2 * T2 + 4
        taps_row = sb("taps_row", [1, KC])
        taps = sb("taps", [P, KC])
        tap_coef = sb("tap_coef", [P, 2, T1 + T2])
        bconv = sb("bconv", [P, 1])
        bfuse = sb("bfuse", [P, 2])
        stats = sb("stats", [P, CT, GROUPS * BN])
        chan = sb("chan", [P, CT, 2])
        grp = sb("grp", [P, CT, 2])
        dev = sb("dev", [P, CT])
        dev2 = sb("dev2", [P, CT])
        var = sb("var", [P, CT])
        std = sb("std", [P, CT])
        rstd = sb("rstd", [P, CT])
        newton = sb("newton", [P, CT])
        rvec = sb("rvec", [P, CT])
        shift_pair = sb("shift_pair", [P, CT, 2])
        bias_f = sb("bias_f", [P, 1])
        gain = sb("gain", [P, 1])
        bias_g = sb("bias_g", [P, 1])

        odd_bank = bank("odd_bank")
        even_bank = bank("even_bank")
        f_bank = bank("f_bank")
        ft_bank = [bank("ft_bank"), bank("gt_bank")]
        y_bank = [bank("y_bank0"), bank("y_bank1")]
        small_bank = bank("small_bank")

        def band_view(b):
            return b[:, 0:2 * BAND].rearrange("p (k r w) -> p k r w", k=2, w=W)

        odd_v, even_v = band_view(odd_bank), band_view(even_bank)

        def band_columns(b):
            return b[:, 0:2 * BAND].rearrange("p (k n) -> p k n", k=2)

        first_loaded = [sem(f"first_loaded{k}") for k in range(GROUPS)]
        x_loaded = sem("x_loaded")
        y_stored = sem("y_stored")
        params_loaded = sem("params_loaded")
        masks_zeroed = sem("masks_zeroed")
        masks_ready = sem("masks_ready")
        setup_mm = sem("setup_mm")
        wconv_ready = sem("wconv_ready")
        wfuse_ready = sem("wfuse_ready")
        bands_ready = sem("bands_ready")
        dve_chain = sem("dve_chain")
        norm_step = sem("norm_step")
        stats_done = sem("stats_done")
        chan_ready = sem("chan_ready")
        grp_done = sem("grp_done")
        dev_ready = sem("dev_ready")
        var_ready = sem("var_ready")
        std_ready = sem("std_ready")
        pair_ready = sem("pair_ready")
        pair_done = sem("pair_done")
        wn_ready = sem("wn_ready")
        bias_ready = sem("bias_ready")
        xh_ready = sem("xh_ready")
        xl_ready = sem("xl_ready")
        f_done = sem("f_done")
        f_ready = sem("f_ready")
        t_done = sem("t_done")
        fth_ready = sem("fth_ready")
        ftl_ready = sem("ftl_ready")
        odd_done = sem("odd_done")
        even_done = sem("even_done")
        oh_ready = sem("oh_ready")
        ol_ready = sem("ol_ready")
        y_done = sem("y_done")
        y_added = sem("y_added")

        block = ctx.enter_context(nc.Block())

        def slot(n):
            return (n % 2) * HW

        def group_no(n, j):
            return GROUPS * n + j

        def odd_split(n, j):
            return O_IMAGE * n + 2 * j + 2

        def even_split(n, j):
            return O_IMAGE * n + 2 * j + 1

        def y_no(n, j, t):
            return Y_IMAGE * n + Y_STEP * j + t + 1

        def loaded(n, j):
            return 16 * (group_no(n, j) - GROUPS + 1)

        @block.sync
        def _(sp):
            def load(n, j, signal):
                at = (GROUPS * n + j) * CHUNK
                sp.dma_start(x_ring[:, :, at:at + CHUNK],
                             x_chunks[n, :, :, j * CHUNK:(j + 1) * CHUNK]).then_inc(signal, 16)

            load(0, 0, first_loaded[0])
            sp.dma_start(wconv_raw[:, :], w_conv).then_inc(params_loaded, 16)
            sp.dma_start(wfuse_raw[:, :, :], w_fuse.rearrange("(h p) c -> p h c", p=P)).then_inc(params_loaded, 16)
            sp.dma_start(bconv[:, :], b_conv.rearrange("(p a) -> p a", a=1)).then_inc(params_loaded, 16)
            for h in range(2):
                sp.dma_start(bfuse[:, h:h + 1], b_fuse[h * P:(h + 1) * P].rearrange("(p a) -> p a", a=1))\
                    .then_inc(params_loaded, 16)
            at = 0
            for v, size in ((wk, T1), (bk, T1), (wk2, T2), (bk2, T2), (wck, 1), (bck, 1), (wck2, 1), (bck2, 1)):
                sp.dma_start(taps_row[:, at:at + size], v.rearrange("(a n) -> a n", a=1)).then_inc(params_loaded, 16)
                at += size
            for k in range(1, GROUPS):
                load(0, k, first_loaded[k])
            for k in range(GROUPS, AHEAD):
                load(1, k - GROUPS, x_loaded)
                sp.wait_ge(x_loaded, loaded(1, k - GROUPS))

            START = 16 * (AHEAD - GROUPS)
            sp.sem_inc(y_stored, START)

            def store(k, earlier=True):
                n, j = k // GROUPS, k % GROUPS
                sp.wait_ge(y_added, Y_BANKS + y_no(n, j + 1, Y_STEP - 1))
                if earlier:
                    sp.wait_ge(y_stored, 16 * k + START)
                    sp.wait_ge(x_loaded, 16 * k + START if loads else START + 16 * (CHUNKS - AHEAD))
                sp.dma_start(out_chunks[n, :, :, bass.ds(j * CHUNK, CHUNK)],
                             x_ring[:, :, bass.ds((k % RING) * CHUNK, CHUNK)]).then_inc(y_stored, 16)

            def load_ahead(k):
                m = k + AHEAD
                sp.dma_start(x_ring[:, :, bass.ds((m % RING) * CHUNK, CHUNK)],
                             x_chunks[m // GROUPS, :, :, bass.ds(m % GROUPS * CHUNK, CHUNK)]).then_inc(x_loaded, 16)

            loads = True
            store(0, earlier=False)
            load_ahead(0)
            with sp.Fori(1, CHUNKS - AHEAD) as k:
                store(k)
                load_ahead(k)
            loads = False
            with sp.Fori(CHUNKS - AHEAD, CHUNKS) as k:
                store(k)
            sp.wait_ge(y_stored, START + 16 * CHUNKS)

        @block.gpsimd
        def _(pool):
            pool.memset(ident[:, :], 0.0).then_inc(masks_zeroed, 1)
            pool.memset(shifts[:, :, :], 0.0).then_inc(masks_zeroed, 1)
            pool.memset(group_avg[:, :], 1.0 / CPG).then_inc(masks_zeroed, 1)
            pool.memset(ones[:, :], 1.0).then_inc(masks_ready, 1)
            pool.wait_ge(masks_zeroed, 3)
            pool.affine_select(out=ident[:, :], in_=ident[:, :], compare_op=ALU.not_equal, fill=1.0,
                               base=0, pattern=[[-1, P]], channel_multiplier=1).then_inc(masks_ready, 1)
            inner = shifts[0:TILE, 2 * HALO:2 * HALO + GROUP_ROWS, 2 * HALO:2 * HALO + TILE_COLS]
            pool.affine_select(out=inner, in_=inner, compare_op=ALU.not_equal, fill=1.0, base=0,
                               pattern=[[TILE_COLS, GROUP_ROWS], [1, TILE_COLS]],
                               channel_multiplier=-1).then_inc(masks_ready, 1)
            ga = group_avg[:, :].rearrange("p (g e) -> p g e", e=CPG)
            pool.affine_select(out=ga, in_=ga, compare_op=ALU.is_ge, fill=0.0, base=0,
                               pattern=[[-CPG, P // CPG], [0, CPG]], channel_multiplier=1).then_inc(masks_zeroed, 1)
            pool.wait_ge(masks_zeroed, 4)
            pool.affine_select(out=ga, in_=ga, compare_op=ALU.is_ge, fill=0.0, base=CPG - 1,
                               pattern=[[CPG, P // CPG], [0, CPG]], channel_multiplier=-1).then_inc(masks_ready, 1)

            def split_x(n, j, at):
                for t in range(CT):
                    pool.wait_ge(xh_ready, CT * group_no(n, j) + t + 1)
                    pool.tensor_tensor(x_lo[:, t, :], x_ring[:, t, bass.ds(at, CHUNK)],
                                       x_hi[:, t, :].bitcast(F32), ALU.subtract).then_inc(xl_ready, 1)

            def image(n, final):
                here, there = pool.snap(slot(n)), pool.snap(slot(n + 1))
                split_x(n, 2, here + 2 * CHUNK)
                with pool.Fori(0, 4) as jj:
                    split_x(n, jj + 3, here + (jj + 3) * CHUNK)
                if not final:
                    split_x(n + 1, 0, there)
                    split_x(n + 1, 1, there + CHUNK)

            split_x(0, 0, 0)
            split_x(0, 1, CHUNK)
            with pool.Fori(0, N - 1) as n:
                image(n, False)
            image(N - 1, True)

        @block.scalar
        def _(act):
            def root(n):
                act.wait_ge(var_ready, n + 1)
                nc.scalar.activation(std[:, :], var[:, :], ACT.Sqrt).then_inc(std_ready, 1)

            def round_x(at):
                for t in range(CT):
                    nc.scalar.activation(x_hi[:, t, :], x_ring[:, t, bass.ds(at, CHUNK)],
                                         ACT.Copy).then_inc(xh_ready, 1)

            def make_f(g):
                act.wait_ge(f_done, g + 1)
                by_rows = f_bank[:, 0:CHUNK].rearrange("p (r q c) -> p r q c", q=TILES, c=TILE_COLS)
                by_tiles = [f_row[:, a, :, :].rearrange("p q (r c) -> p r q c", c=TILE_COLS) for a in range(2)]
                nc.scalar.activation(by_tiles[0], by_rows, ACT.Relu,
                                     bias=bias_f[:, 0:1]).then_inc(f_ready, 1)
                nc.scalar.activation(by_tiles[1], by_rows, ACT.Relu,
                                     bias=bias_g[:, 0:1], scale=gain[:, 0:1]).then_inc(f_ready, 1)

            def round_ft(g, parity):
                for a in range(2):
                    act.wait_ge(t_done, 2 * g + a + 1)
                    nc.scalar.activation(ft_hi[0:TILE, parity, a, :], ft_bank[a][0:TILE, :],
                                         ACT.Copy).then_inc(fth_ready, 1)

            def round_band(b, to):
                nc.scalar.activation(o_hi[:, to, :, :], band_columns(b), ACT.Copy).then_inc(oh_ready, 1)

            def step(n, j, parity, here, there, first=False, last=False, chain=False, after=None):
                g = group_no(n, j)
                if not first:
                    act.wait_ge(odd_done, g)
                    round_band(odd_bank, ODD)
                act.wait_ge(even_done, g + 1)
                round_band(even_bank, EVEN)
                if after is not None:
                    if last:
                        act.wait_ge(bias_ready, n + 2)
                    make_f(g + 1)
                    if not (last or chain):
                        round_x(here + (j + 2) * CHUNK)
                    elif "split" in after:
                        if chain:
                            act.wait_ge(x_loaded, loaded(n + 1, 0))
                            round_x(there)
                        else:
                            act.wait_ge(x_loaded, loaded(n + 1, 1))
                            round_x(there + CHUNK)
                if last:
                    act.wait_ge(odd_done, g + 1)
                    round_band(odd_bank, TAIL)
                if after is not None:
                    round_ft(g + 1, parity)
                if chain and "split" in after:
                    root(n + 1)

            def image(n, final):
                here, there = act.snap(slot(n)), act.snap(slot(n + 1))
                step(n, 0, 1, here, there, first=True, after="f split")
                with act.Fori(0, 2) as jj:
                    step(n, 2 * jj + 1, 0, here, there, after="f split")
                    step(n, 2 * jj + 2, 1, here, there, after="f split")
                step(n, 5, 0, here, there, chain=True, after="f" if final else "f split")
                step(n, 6, 0, here, there, last=True, after=None if final else "f split")

            act.wait_ge(first_loaded[0], 16)
            round_x(0)
            root(0)
            act.wait_ge(bias_ready, 1)
            make_f(0)
            act.wait_ge(first_loaded[1], 16)
            round_x(CHUNK)
            round_ft(0, 0)
            with act.Fori(0, N - 1) as n:
                image(n, False)
            image(N - 1, True)

        @block.vector
        def _(dve):
            links = [0]

            def link(ins):
                links[0] += 1
                ins.then_inc(dve_chain, 1)
                dve.wait_ge(dve_chain, links[0])

            nc.vector.memset(newton[:, :], 0.0).then_inc(y_added, Y_BANKS)

            dve.wait_ge(setup_mm, 1)
            link(nc.vector.tensor_copy(taps[:, :], small_bank[:, 0:KC]))
            s = 2 * T1 + 2 * T2
            for at, a0, b0, T, k in ((0, 0, T1, T1, s), (T1, 2 * T1, 2 * T1 + T2, T2, s + 2)):
                nc.vector.tensor_scalar(tap_coef[:, 1, at:at + T], taps[:, a0:a0 + T], taps[:, k:k + 1],
                                        None, ALU.mult)
                link(nc.vector.tensor_scalar(tap_coef[:, 0, at:at + T], taps[:, b0:b0 + T], taps[:, k:k + 1],
                                             taps[:, k + 1:k + 2], ALU.mult, ALU.add))

            dve.wait_ge(setup_mm, 2)
            nc.vector.tensor_copy(wconv_t[:, :, :],
                                  y_bank[0][:, :].rearrange("p (t o) -> p t o", t=CT)).then_inc(wconv_ready, 1)
            dve.wait_ge(setup_mm, 3)
            link(nc.vector.tensor_copy(wfuse_t[:, :, :], y_bank[1][:, 0:2 * P].rearrange("p (h o) -> p h o", h=2)))
            link(nc.vector.tensor_copy(wfuse_hi[:, :, :], wfuse_t[:, :, :]))
            nc.vector.tensor_tensor(wfuse_lo[:, :, :], wfuse_t[:, :, :], wfuse_hi[:, :, :].bitcast(F32),
                                    ALU.subtract).then_inc(wfuse_ready, 1)

            def channel_stats(at, k):
                for t in range(CT):
                    ins = nc.vector.bn_stats(stats[:, t, bass.ds(BN * k, BN)], x_ring[:, t, bass.ds(at, CHUNK)])
                return ins

            def small(ins, n, k):
                ins.then_inc(norm_step, 1)
                dve.wait_ge(norm_step, NORM_STEPS * n + k)

            def norm_channels(n):
                dve.wait_ge(stats_done, 2 * n + 2)
                nc.vector.memset(newton[:, :], 0.0)
                for t in range(CT):
                    ins = nc.vector.bn_aggr(chan[:, t, :], stats[:, t, :])
                ins.then_inc(chan_ready, 1)

            def norm_deviations(n):
                dve.wait_ge(grp_done, 2 * n + 1)
                small(nc.vector.tensor_copy(grp[:, :, :], small_bank[:, 0:2 * CT].rearrange("p (t s) -> p t s", s=2)),
                      n, 1)
                small(nc.vector.tensor_tensor(dev[:, :], chan[:, :, 0], grp[:, :, 0], ALU.subtract), n, 2)
                nc.vector.tensor_tensor(dev2[:, :], dev[:, :], dev[:, :], ALU.mult).then_inc(dev_ready, 1)

            def norm_weights(n):
                dve.wait_ge(grp_done, 2 * n + 2)
                nc.vector.scalar_tensor_tensor(var[:, :], small_bank[:, VAR_AT:VAR_AT + CT], EPS, grp[:, :, 1],
                                               ALU.add, ALU.add).then_inc(var_ready, 1)
                dve.wait_ge(std_ready, n + 1)
                small(nc.vector.reciprocal(rstd[:, :], std[:, :]), n, 3)
                small(nc.vector.tensor_tensor(newton[:, :], rstd[:, :], rstd[:, :], ALU.mult), n, 4)
                small(nc.vector.tensor_tensor(newton[:, :], newton[:, :], var[:, :], ALU.mult), n, 5)
                small(nc.vector.tensor_scalar(newton[:, :], newton[:, :], -0.5, 1.5, ALU.mult, ALU.add), n, 6)
                small(nc.vector.tensor_tensor(rvec[:, :], newton[:, :], rstd[:, :], ALU.mult), n, 7)
                nc.vector.scalar_tensor_tensor(shift_pair[:, :, 0], grp[:, :, 0], -1.0, rvec[:, :],
                                               ALU.mult, ALU.mult)
                nc.vector.tensor_tensor(shift_pair[:, :, 1], dev[:, :], rvec[:, :], ALU.mult).then_inc(pair_ready, 1)
                for t in range(CT):
                    ins = nc.vector.tensor_scalar(wn[:, t, :], wconv_t[:, t, :], rvec[:, t:t + 1], None, ALU.mult)
                small(ins, n, 8)
                small(nc.vector.tensor_copy(wn_hi[:, :, :], wn[:, :, :]), n, 9)
                nc.vector.tensor_tensor(wn_lo[:, :, :], wn[:, :, :], wn_hi[:, :, :].bitcast(F32),
                                        ALU.subtract).then_inc(wn_ready, 1)

            def norm_biases(n):
                dve.wait_ge(pair_done, n + 1)
                small(nc.vector.tensor_scalar(bias_f[:, :], small_bank[:, PAIR_AT:PAIR_AT + 1], bconv[:, 0:1],
                                              None, ALU.add), n, 10)
                small(nc.vector.tensor_scalar(gain[:, :], small_bank[:, PAIR_AT + 1:PAIR_AT + 2], bconv[:, 0:1],
                                              0.0, ALU.add, ALU.max), n, 11)
                nc.vector.tensor_tensor(bias_g[:, :], bias_f[:, :], gain[:, :], ALU.mult).then_inc(bias_ready, 1)

            for j in range(GROUPS):
                dve.wait_ge(first_loaded[j], 16)
                ins = channel_stats(j * CHUNK, j)
            ins.then_inc(stats_done, 2)
            norm_channels(0)
            norm_deviations(0)
            norm_weights(0)
            norm_biases(0)

            for k, (width, step_by, first_tap) in enumerate(((K1, 1, 0), (K2, 2, T1))):
                for tap in range(width * width):
                    dr, dc = step_by * (tap // width), step_by * (tap % width)
                    view = shifts[0:TILE, dr:dr + WIN_ROWS, dc:dc + WIN_COLS]
                    for ab in range(2):
                        acc = band_f32[0:TILE, ab, k, :].rearrange("p (r c) -> p r c", c=WIN_COLS)
                        coef = tap_coef[0:TILE, ab, first_tap + tap:first_tap + tap + 1]
                        if tap == 0:
                            ins = nc.vector.tensor_scalar(acc, view, coef, None, ALU.mult)
                        else:
                            ins = nc.vector.scalar_tensor_tensor(acc, view, coef, acc, ALU.mult, ALU.add)
                    link(ins)
            link(nc.vector.tensor_copy(band_hi[0:TILE, :, :, :], band_f32[0:TILE, :, :, :]))
            nc.vector.tensor_tensor(band_lo[0:TILE, :, :, :], band_f32[0:TILE, :, :, :],
                                    band_hi[0:TILE, :, :, :].bitcast(F32), ALU.subtract).then_inc(bands_ready, 1)

            def rest_of_band(b, to, value):
                dve.wait_ge(oh_ready, value)
                nc.vector.tensor_tensor(o_lo[:, to, :, :], band_columns(b), o_hi[:, to, :, :].bitcast(F32),
                                        ALU.subtract).then_inc(ol_ready, 1)

            def rest_of_ft(g, parity):
                for a in range(2):
                    dve.wait_ge(fth_ready, 2 * g + a + 1)
                    nc.vector.tensor_tensor(ft_lo[0:TILE, parity, a, :], ft_bank[a][0:TILE, :],
                                            ft_hi[0:TILE, parity, a, :].bitcast(F32),
                                            ALU.subtract).then_inc(ftl_ready, 1)

            def add_y(n, j, tiles, at, size):
                for t in tiles:
                    dve.wait_ge(y_done, y_no(n, j, t))
                    xs = x_ring[:, t, bass.ds(at, size)]
                    nc.vector.scalar_tensor_tensor(xs, y_bank[t % Y_BANKS][:, 0:size], bfuse[:, t % 2:t % 2 + 1],
                                                   xs, ALU.add, ALU.add).then_inc(y_added, 1)

            def next_stats(n, there, k):
                dve.wait_ge(x_loaded, loaded(n + 1, k))
                return channel_stats(there + k * CHUNK, k)

            def image(n, final):
                here, there = dve.snap(slot(n)), dve.snap(slot(n + 1))
                rest_of_band(even_bank, EVEN, even_split(n, 0))
                if not final:
                    next_stats(n, there, 0)
                add_y(n, 0, (0, 1), here, BAND)
                rest_of_ft(group_no(n, 1), 1)
                add_y(n, 0, (2, 3), here, BAND)
                with dve.Fori(0, 2) as jj:
                    for odd in (1, 0):
                        j = 2 * jj + (1 if odd else 2)
                        at = here + j * CHUNK - BAND
                        rest_of_band(odd_bank, ODD, odd_split(n, j - 1))
                        rest_of_band(even_bank, EVEN, even_split(n, j))
                        if not final:
                            if odd:
                                next_stats(n, there, 3 * jj + 1)
                            else:
                                next_stats(n, there, 3 * jj + 2)
                                next_stats(n, there, 3 * jj + 3).then_inc(stats_done, 1)
                        add_y(n, j, (0, 1), at, CHUNK)
                        rest_of_ft(group_no(n, j) + 1, 1 - odd)
                        add_y(n, j, (2, 3), at, CHUNK)
                rest_of_band(odd_bank, ODD, odd_split(n, 4))
                rest_of_band(even_bank, EVEN, even_split(n, 5))
                if not final:
                    norm_channels(n + 1)
                add_y(n, 5, (0, 1), here + 5 * CHUNK - BAND, CHUNK)
                if not final:
                    norm_deviations(n + 1)
                rest_of_ft(group_no(n, 6), 0)
                add_y(n, 5, (2, 3), here + 5 * CHUNK - BAND, CHUNK)
                if not final:
                    norm_weights(n + 1)
                rest_of_band(odd_bank, ODD, odd_split(n, 5))
                rest_of_band(even_bank, EVEN, even_split(n, 6))
                if not final:
                    norm_biases(n + 1)
                add_y(n, 6, (0, 1), here + 6 * CHUNK - BAND, CHUNK)
                rest_of_band(odd_bank, TAIL, odd_split(n, 6))
                if not final:
                    rest_of_ft(group_no(n + 1, 0), 0)
                add_y(n, 6, (2, 3), here + 6 * CHUNK - BAND, CHUNK)
                add_y(n, GROUPS, range(CT), here + HW - BAND, BAND)

            rest_of_ft(0, 0)
            with dve.Fori(0, N - 1) as n:
                image(n, False)
            image(N - 1, True)

        @block.tensor
        def _(pe):
            def three(dst, w, m, start, stop, check=True):
                nc.tensor.matmul(dst, w[0], m[0], start=start, stop=False, skip_group_check=not check)
                nc.tensor.matmul(dst, w[0], m[1], start=False, stop=False, skip_group_check=not check)
                return nc.tensor.matmul(dst, w[1], m[0], start=False, stop=stop, skip_group_check=not check)

            pe.wait_ge(params_loaded, 16 * 13)
            pe.wait_ge(masks_ready, 4)
            nc.tensor.matmul(small_bank[:, 0:KC], ones[:, :], taps_row[:, :], start=True, stop=True)\
                .then_inc(setup_mm, 1)
            for t in range(CT):
                ins = nc.tensor.transpose(y_bank[0][:, t * CM:(t + 1) * CM], wconv_raw[:, t * P:(t + 1) * P],
                                          ident[:, :])
            ins.then_inc(setup_mm, 1)
            for h in range(2):
                ins = nc.tensor.transpose(y_bank[1][:, h * P:(h + 1) * P], wfuse_raw[:, h, :], ident[:, :])
            ins.then_inc(setup_mm, 1)

            def average_channels(n):
                pe.wait_ge(chan_ready, n + 1)
                nc.tensor.matmul(small_bank[:, 0:2 * CT], group_avg[:, :], chan[:, :, :],
                                 start=True, stop=True).then_inc(grp_done, 1)

            def average_deviations(n):
                pe.wait_ge(dev_ready, n + 1)
                nc.tensor.matmul(small_bank[:, VAR_AT:VAR_AT + CT], group_avg[:, :], dev2[:, :],
                                 start=True, stop=True).then_inc(grp_done, 1)

            def conv_of_pair(n):
                pe.wait_ge(pair_ready, n + 1)
                for t in range(CT):
                    ins = nc.tensor.matmul(small_bank[:, PAIR_AT:PAIR_AT + 2], wconv_t[:, t, :], shift_pair[:, t, :],
                                           start=t == 0, stop=t == CT - 1)
                ins.then_inc(pair_done, 1)

            def conv_in(g):
                if not isinstance(g, int) or g > 0:
                    pe.wait_ge(f_ready, 2 * g)
                for t in range(CT):
                    pe.wait_ge(xl_ready, CT * g + t + 1)
                    ins = three(f_bank[:, 0:CHUNK], (wn_hi[:, t, :], wn_lo[:, t, :]),
                                (x_hi[:, t, :], x_lo[:, t, :]), t == 0, t == CT - 1)
                ins.then_inc(f_done, 1)

            def transposes(g):
                for a in range(2):
                    pe.wait_ge(f_ready, 2 * g + a + 1)
                    for q in range(TILES):
                        ins = nc.tensor.transpose(ft_bank[a][0:TILE, q * CM:(q + 1) * CM],
                                                  f_row[:, a, q, :], ident[:, :])
                    ins.then_inc(t_done, 1)

            def bands(view, to_row, win_row, rows, parity, fresh):
                for a in range(2):
                    for q in range(TILES):
                        lo, hi, c0, c1 = window(q)
                        chans = slice(q * CM, (q + 1) * CM)
                        w = (ft_hi[0:TILE, parity, a, chans], ft_lo[0:TILE, parity, a, chans])
                        m = [b[0:TILE, a, :, :].rearrange("p k (r c) -> p k r c", c=WIN_COLS)
                             [:, :, win_row:win_row + rows, c0:c1] for b in (band_hi, band_lo)]
                        ins = three(view[:, :, to_row:to_row + rows, lo:hi], w, m,
                                    fresh and a == 0 and q == 0, a == 1 and q == TILES - 1, check=False)
                return ins

            def fuse(n, j, tiles, slots):
                for t in tiles:
                    k, h = t // 2, t % 2
                    pe.wait_ge(y_added, y_no(n, j, t))
                    dst = y_bank[t % Y_BANKS][:, 0:BAND * len(slots)]
                    m = [o[:, slots[0]:slots[-1] + 1, k, :] for o in (o_hi, o_lo)]
                    three(dst, (wfuse_hi[:, h, :], wfuse_lo[:, h, :]), m, True, True).then_inc(y_done, 1)

            def step(n, j, parity, first=False, last=False, norm=False, more=True):
                g = group_no(n, j)
                pe.wait_ge(ftl_ready, 2 * g + 2)
                if not first:
                    bands(odd_v, BAND_ROWS - HALO, 0, HALO, parity, False).then_inc(odd_done, 1)
                if last and norm:
                    conv_of_pair(n + 1)
                bands(even_v, 0, HALO, BAND_ROWS, parity, first).then_inc(even_done, 1)
                if more:
                    if last:
                        pe.wait_ge(wn_ready, n + 2)
                    conv_in(g + 1)
                if not first:
                    pe.wait_ge(ol_ready, odd_split(n, j - 1))
                ins = bands(odd_v, 0, HALO + BAND_ROWS, BAND_ROWS, parity, True)
                if last:
                    ins.then_inc(odd_done, 1)
                pe.wait_ge(ol_ready, even_split(n, j))
                slots = (EVEN,) if first else (ODD, EVEN)
                fuse(n, j, (0, 1), slots)
                if norm and not last:
                    average_channels(n + 1)
                if more:
                    transposes(g + 1)
                if not last:
                    bands(even_v, 0, HALO + 2 * BAND_ROWS, HALO, parity, True)
                if norm and not last:
                    average_deviations(n + 1)
                fuse(n, j, (2, 3), slots)
                if last:
                    pe.wait_ge(ol_ready, odd_split(n, j))
                    fuse(n, GROUPS, range(CT), (TAIL,))

            def image(n, final):
                step(n, 0, 0, first=True)
                with pe.Fori(0, 2) as jj:
                    step(n, 2 * jj + 1, 1)
                    step(n, 2 * jj + 2, 0)
                step(n, 5, 1, norm=not final)
                step(n, 6, 0, last=True, norm=not final, more=not final)

            average_channels(0)
            average_deviations(0)
            conv_of_pair(0)
            pe.wait_ge(wn_ready, 1)
            conv_in(0)
            transposes(0)
            pe.wait_ge(wfuse_ready, 1)
            pe.wait_ge(bands_ready, 1)
            with pe.Fori(0, N - 1) as n:
                image(n, False)
            image(N - 1, True)


_INS = ["x"] + ["L0_conv_" + k for k in
                ("W_conv", "b_conv", "wk", "bk", "wck", "bck", "wk2", "bk2", "wck2", "bck2", "W_fuse", "b_fuse")]


def kernel(**inputs):
    import numpy as _np
    import concourse.bacc as _bacc
    from concourse import mybir as _mybir
    from concourse.bass_utils import run_bass_kernel_spmd as _run

    nc = _bacc.Bacc("TRN2", target_bir_lowering=False, num_devices=1)
    arrays, args = {}, []
    for name in _INS:
        a = _np.ascontiguousarray(inputs[name])
        a = a.reshape(a.shape or (1,))
        arrays[f"in_{name}_dram"] = a
        args.append(nc.dram_tensor(f"in_{name}_dram", a.shape, _mybir.dt.from_np(a.dtype), kind="ExternalInput").ap())
    shape = tuple(inputs["x"].shape)
    args.append(nc.dram_tensor("out_0_dram", shape, _mybir.dt.float32, kind="ExternalOutput").ap())
    build(nc, *args)
    r = _run(nc, [arrays], core_ids=[0])
    return r.results[0]["out_0_dram"]
```

```python
from contextlib import ExitStack

import concourse.bass as bass
from concourse import mybir

ALU = mybir.AluOpType
ACT = mybir.ActivationFunctionType
AX = mybir.AxisListType
F32 = mybir.dt.float32
F32R = mybir.dt.float32r
F16 = mybir.dt.float16
U32 = mybir.dt.uint32

P = 128
N, C, H, W = 32, 512, 56, 56
CM = 128
CT = C // P
CPG = 16
EPS = 1e-5
K1, K2 = 5, 3
HALO = 2
HW = H * W

GROUP_ROWS = 8
GROUPS = H // GROUP_ROWS
CHUNK = GROUP_ROWS * W
BAND_ROWS = GROUP_ROWS // 2
BAND = BAND_ROWS * W
TILE_ROWS, TILE_COLS = 4, 28
TILE = TILE_ROWS * TILE_COLS
ROW_BLOCKS = GROUP_ROWS // TILE_ROWS
COL_BLOCKS = W // TILE_COLS
TILES = ROW_BLOCKS * COL_BLOCKS
WIN_ROWS = TILE_ROWS + 2 * HALO
WIN_COLS = TILE_COLS + 2 * HALO
WIN = WIN_ROWS * WIN_COLS

RING = 2 * GROUPS
AHEAD = RING - 1
CHUNKS = N * GROUPS

BN = 6
Y_BANKS = 2
Y_STEP = CT
Y_EDGE = CT // 2
Y_IMAGE = Y_STEP * (GROUPS - 1) + 2 * Y_EDGE
O_IMAGE = 2 * GROUPS
VAR_AT, PAIR_AT = 2 * CT, 16
NORM_STEPS = 11
ODD, EVEN, TAIL = range(3)


SPLIT = 2.0 ** 11
TOP = 2.0 ** 14
XN_MAX = (CPG * HW) ** 0.5
XN_MEAN_MAX = CPG ** 0.5
TINY = 2.0 ** -60


def window(q):
    left, right = TILE_COLS * q - HALO, TILE_COLS * (q + 1) + HALO
    lo, hi = max(left, 0), min(right, W)
    return lo, hi, lo - left, hi - left


def share(b, band_row):
    top = TILE_ROWS * b - HALO
    lo, hi = max(top, band_row), min(top + WIN_ROWS, band_row + BAND_ROWS)
    return lo - band_row, lo - top, hi - lo


def build(nc, x, w_conv, b_conv, wk, bk, wck, bck, wk2, bk2, wck2, bck2, w_fuse, b_fuse, out):
    x_chunks = x.rearrange("n (t p) h w -> n p t (h w)", p=P)
    out_chunks = out.rearrange("n (t p) h w -> n p t (h w)", p=P)

    with ExitStack() as ctx:
        def sb(name, shape, dt=F32):
            return ctx.enter_context(nc.sbuf_tensor(name, shape, dt))

        def bank(name):
            return ctx.enter_context(nc.psum_tensor(name, [P, 512], F32))

        def sem(name):
            return ctx.enter_context(nc.semaphore(name))

        x_ring = sb("x_ring", [P, CT, RING * CHUNK])
        x_hi = sb("x_hi", [P, CT, CHUNK], F32R)
        x_lo = sb("x_lo", [P, CT, CHUNK], F32R)
        f_row = sb("f_row", [P, 2, COL_BLOCKS, ROW_BLOCKS * TILE])
        ft_hi = sb("ft_hi", [P, 2, 2, TILES * CM], F16)
        ft_lo = sb("ft_lo", [P, 2, 2, TILES * CM], F16)
        o_hi = sb("o_hi", [P, 3, 2, BAND], F32R)
        o_lo = sb("o_lo", [P, 3, 2, BAND], F32R)
        band_hi = sb("band_hi", [P, 2, 2, WIN], F16)
        band_lo = sb("band_lo", [P, 2, 2, WIN], F16)
        band_hi_down = sb("band_hi_down", [P, 2, 2, WIN], F16)
        band_f32 = sb("band_f32", [P, 2, 2, WIN])
        shifts = sb("shifts", [P, WIN_ROWS + 2 * HALO, WIN_COLS + 2 * HALO])
        wconv_raw = sb("wconv_raw", [P, C])
        wfuse_raw = sb("wfuse_raw", [P, 2, CM])
        wconv_t = sb("wconv_t", [P, CT, CM])
        wn = sb("wn", [P, CT, CM])
        wn_hi = sb("wn_hi", [P, CT, CM], F32R)
        wn_lo = sb("wn_lo", [P, CT, CM], F32R)
        wfuse_t = sb("wfuse_t", [P, 2, P])
        wfuse_hi = sb("wfuse_hi", [P, 2, P], F32R)
        wfuse_lo = sb("wfuse_lo", [P, 2, P], F32R)
        ident = sb("ident", [P, P])
        group_avg = sb("group_avg", [P, P])
        ones = sb("ones", [1, P])
        T1, T2 = K1 * K1, K2 * K2
        KC = 2 * T1 + 2 * T2 + 4
        taps_row = sb("taps_row", [1, KC])
        taps = sb("taps", [P, KC])
        tap_coef = sb("tap_coef", [P, 2, T1 + T2])
        bconv = sb("bconv", [P, 1])
        bfuse = sb("bfuse", [P, 2])
        stats = sb("stats", [P, CT, GROUPS * BN])
        chan = sb("chan", [P, CT, 2])
        grp = sb("grp", [P, CT, 2])
        dev = sb("dev", [P, CT])
        dev2 = sb("dev2", [P, CT])
        var = sb("var", [P, CT])
        std = sb("std", [P, CT])
        rstd = sb("rstd", [P, CT])
        newton = sb("newton", [P, CT])
        rvec = sb("rvec", [P, CT])
        shift_pair = sb("shift_pair", [P, CT, 2])
        wsq = sb("wsq", [P, C])
        wnorm2 = sb("wnorm2", [P, C // CPG])
        wnorm = sb("wnorm", [P, C // CPG])
        wreach = sb("wreach", [P, 1])
        babs = sb("babs", [P, 1])
        bound = sb("bound", [P, 4])
        tap_abs = sb("tap_abs", [P, 2, T1 + T2])
        f_scale = sb("f_scale", [P, 1])
        tap_scale = sb("tap_scale", [P, 1])
        o_scale = sb("o_scale", [P, 1])
        bias_f = sb("bias_f", [P, 1])
        gain = sb("gain", [P, 1])
        gain_f = sb("gain_f", [P, 1])
        bias_g = sb("bias_g", [P, 1])

        odd_bank = bank("odd_bank")
        even_bank = bank("even_bank")
        f_bank = bank("f_bank")
        ft_bank = [bank("ft_bank"), bank("gt_bank")]
        y_bank = [bank("y_bank0"), bank("y_bank1")]
        small_bank = bank("small_bank")

        def band_view(b):
            return b[:, 0:2 * BAND].rearrange("p (k r w) -> p k r w", k=2, w=W)

        odd_v, even_v = band_view(odd_bank), band_view(even_bank)

        def band_columns(b):
            return b[:, 0:2 * BAND].rearrange("p (k n) -> p k n", k=2)

        first_loaded = [sem(f"first_loaded{k}") for k in range(GROUPS)]
        x_loaded = sem("x_loaded")
        y_stored = sem("y_stored")
        params_loaded = sem("params_loaded")
        masks_zeroed = sem("masks_zeroed")
        masks_ready = sem("masks_ready")
        setup_mm = sem("setup_mm")
        wconv_ready = sem("wconv_ready")
        wfuse_ready = sem("wfuse_ready")
        wnorm2_ready = sem("wnorm2_ready")
        wnorm_ready = sem("wnorm_ready")
        bands_ready = sem("bands_ready")
        dve_chain = sem("dve_chain")
        norm_step = sem("norm_step")
        stats_done = sem("stats_done")
        chan_ready = sem("chan_ready")
        grp_done = sem("grp_done")
        dev_ready = sem("dev_ready")
        var_ready = sem("var_ready")
        std_ready = sem("std_ready")
        pair_ready = sem("pair_ready")
        pair_done = sem("pair_done")
        wn_ready = sem("wn_ready")
        bias_ready = sem("bias_ready")
        xh_ready = sem("xh_ready")
        xl_ready = sem("xl_ready")
        f_done = sem("f_done")
        f_ready = sem("f_ready")
        t_done = sem("t_done")
        fth_ready = sem("fth_ready")
        ftl_ready = sem("ftl_ready")
        odd_done = sem("odd_done")
        even_done = sem("even_done")
        oh_ready = sem("oh_ready")
        ol_ready = sem("ol_ready")
        y_done = sem("y_done")
        y_added = sem("y_added")

        block = ctx.enter_context(nc.Block())

        def slot(n):
            return (n % 2) * HW

        def group_no(n, j):
            return GROUPS * n + j

        def odd_split(n, j):
            return O_IMAGE * n + 2 * j + 2

        def even_split(n, j):
            return O_IMAGE * n + 2 * j + 1

        def y_no(n, j, t):
            return Y_IMAGE * n + Y_STEP * (j - 1) + Y_EDGE + t + 1

        def y_first(n, t):
            return Y_IMAGE * n + t + 1

        def loaded(n, j):
            return 16 * (group_no(n, j) - GROUPS + 1)

        @block.sync
        def _(sp):
            def load(n, j, signal):
                at = (GROUPS * n + j) * CHUNK
                sp.dma_start(x_ring[:, :, at:at + CHUNK],
                             x_chunks[n, :, :, j * CHUNK:(j + 1) * CHUNK]).then_inc(signal, 16)

            load(0, 0, first_loaded[0])
            sp.dma_start(wconv_raw[:, :], w_conv).then_inc(params_loaded, 16)
            sp.dma_start(wfuse_raw[:, :, :], w_fuse.rearrange("(h p) c -> p h c", p=P)).then_inc(params_loaded, 16)
            sp.dma_start(bconv[:, :], b_conv.rearrange("(p a) -> p a", a=1)).then_inc(params_loaded, 16)
            for h in range(2):
                sp.dma_start(bfuse[:, h:h + 1], b_fuse[h * P:(h + 1) * P].rearrange("(p a) -> p a", a=1))\
                    .then_inc(params_loaded, 16)
            at = 0
            for v, size in ((wk, T1), (bk, T1), (wk2, T2), (bk2, T2), (wck, 1), (bck, 1), (wck2, 1), (bck2, 1)):
                sp.dma_start(taps_row[:, at:at + size], v.rearrange("(a n) -> a n", a=1)).then_inc(params_loaded, 16)
                at += size
            for k in range(1, GROUPS):
                load(0, k, first_loaded[k])
            for k in range(GROUPS, AHEAD):
                load(1, k - GROUPS, x_loaded)
                sp.wait_ge(x_loaded, loaded(1, k - GROUPS))

            START = 16 * (AHEAD - GROUPS)
            sp.sem_inc(y_stored, START)

            def store(k, earlier=True):
                n, j = k // GROUPS, k % GROUPS
                if isinstance(k, int) and k == CHUNKS - 1:
                    sp.wait_ge(y_added, Y_BANKS + Y_IMAGE * N)
                else:
                    sp.wait_ge(y_added, Y_BANKS + y_no(n, j + 1, Y_STEP - 1))
                if earlier:
                    sp.wait_ge(y_stored, 16 * k + START)
                    sp.wait_ge(x_loaded, 16 * k + START if loads else START + 16 * (CHUNKS - AHEAD))
                sp.dma_start(out_chunks[n, :, :, bass.ds(j * CHUNK, CHUNK)],
                             x_ring[:, :, bass.ds((k % RING) * CHUNK, CHUNK)]).then_inc(y_stored, 16)

            def load_ahead(k):
                m = k + AHEAD
                sp.dma_start(x_ring[:, :, bass.ds((m % RING) * CHUNK, CHUNK)],
                             x_chunks[m // GROUPS, :, :, bass.ds(m % GROUPS * CHUNK, CHUNK)]).then_inc(x_loaded, 16)

            loads = True
            store(0, earlier=False)
            load_ahead(0)
            with sp.Fori(1, CHUNKS - AHEAD) as k:
                store(k)
                load_ahead(k)
            loads = False
            with sp.Fori(CHUNKS - AHEAD, CHUNKS - 1) as k:
                store(k)
            store(CHUNKS - 1)
            sp.wait_ge(y_stored, START + 16 * CHUNKS)

        @block.gpsimd
        def _(pool):
            pool.memset(ident[:, :], 0.0).then_inc(masks_zeroed, 1)
            pool.memset(shifts[:, :, :], 0.0).then_inc(masks_zeroed, 1)
            pool.memset(group_avg[:, :], 1.0 / CPG).then_inc(masks_zeroed, 1)
            pool.memset(ones[:, :], 1.0).then_inc(masks_ready, 1)
            pool.wait_ge(masks_zeroed, 3)
            pool.affine_select(out=ident[:, :], in_=ident[:, :], compare_op=ALU.not_equal, fill=1.0,
                               base=0, pattern=[[-1, P]], channel_multiplier=1).then_inc(masks_ready, 1)
            inner = shifts[0:TILE, 2 * HALO:2 * HALO + TILE_ROWS, 2 * HALO:2 * HALO + TILE_COLS]
            pool.affine_select(out=inner, in_=inner, compare_op=ALU.not_equal, fill=1.0, base=0,
                               pattern=[[TILE_COLS, TILE_ROWS], [1, TILE_COLS]],
                               channel_multiplier=-1).then_inc(masks_ready, 1)
            ga = group_avg[:, :].rearrange("p (g e) -> p g e", e=CPG)
            pool.affine_select(out=ga, in_=ga, compare_op=ALU.is_ge, fill=0.0, base=0,
                               pattern=[[-CPG, P // CPG], [0, CPG]], channel_multiplier=1).then_inc(masks_zeroed, 1)
            pool.wait_ge(masks_zeroed, 4)
            pool.affine_select(out=ga, in_=ga, compare_op=ALU.is_ge, fill=0.0, base=CPG - 1,
                               pattern=[[CPG, P // CPG], [0, CPG]], channel_multiplier=-1).then_inc(masks_ready, 1)

            def split_x(n, j, at):
                for t in range(CT):
                    pool.wait_ge(xh_ready, CT * group_no(n, j) + t + 1)
                    pool.tensor_tensor(x_lo[:, t, :], x_ring[:, t, bass.ds(at, CHUNK)],
                                       x_hi[:, t, :].bitcast(F32), ALU.subtract).then_inc(xl_ready, 1)

            def image(n, final):
                here, there = pool.snap(slot(n)), pool.snap(slot(n + 1))
                split_x(n, 2, here + 2 * CHUNK)
                with pool.Fori(0, 4) as jj:
                    split_x(n, jj + 3, here + (jj + 3) * CHUNK)
                if not final:
                    split_x(n + 1, 0, there)
                    split_x(n + 1, 1, there + CHUNK)

            split_x(0, 0, 0)
            split_x(0, 1, CHUNK)
            with pool.Fori(0, N - 1) as n:
                image(n, False)
            image(N - 1, True)

        @block.scalar
        def _(act):
            def root(n):
                act.wait_ge(var_ready, n + 1)
                nc.scalar.activation(std[:, :], var[:, :], ACT.Sqrt).then_inc(std_ready, 1)

            def round_x(at):
                for t in range(CT):
                    nc.scalar.activation(x_hi[:, t, :], x_ring[:, t, bass.ds(at, CHUNK)],
                                         ACT.Copy).then_inc(xh_ready, 1)

            def make_f(g):
                act.wait_ge(f_done, g + 1)
                by_rows = f_bank[:, 0:CHUNK].rearrange("p (r q c) -> p r q c", q=COL_BLOCKS, c=TILE_COLS)
                by_tiles = [f_row[:, a, :, :].rearrange("p q (r c) -> p r q c", c=TILE_COLS) for a in range(2)]
                nc.scalar.activation(by_tiles[0], by_rows, ACT.Relu,
                                     bias=bias_f[:, 0:1], scale=f_scale[:, 0:1]).then_inc(f_ready, 1)
                nc.scalar.activation(by_tiles[1], by_rows, ACT.Relu,
                                     bias=bias_g[:, 0:1], scale=gain_f[:, 0:1]).then_inc(f_ready, 1)

            def round_ft(g, parity):
                for a in range(2):
                    act.wait_ge(t_done, 2 * g + a + 1)
                    nc.scalar.activation(ft_hi[0:TILE, parity, a, :], ft_bank[a][0:TILE, :],
                                         ACT.Copy, scale=1.0 / SPLIT).then_inc(fth_ready, 1)

            def round_band(b, to):
                nc.scalar.activation(o_hi[:, to, :, :], band_columns(b), ACT.Copy,
                                     scale=o_scale[:, 0:1]).then_inc(oh_ready, 1)

            def step(n, j, parity, here, there, first=False, last=False, norm=None, more=True):
                g = group_no(n, j)
                if not first:
                    act.wait_ge(odd_done, g)
                    round_band(odd_bank, ODD)
                act.wait_ge(even_done, g + 1)
                round_band(even_bank, EVEN)
                if last:
                    if more:
                        act.wait_ge(bias_ready, n + 2)
                        make_f(g + 1)
                    act.wait_ge(odd_done, g + 1)
                    round_band(odd_bank, TAIL)
                    if more:
                        act.wait_ge(x_loaded, loaded(n + 1, 1))
                        round_x(there + CHUNK)
                elif norm is None:
                    make_f(g + 1)
                    round_x(here + (j + 2) * CHUNK)
                else:
                    make_f(g + 1)
                    if norm:
                        act.wait_ge(x_loaded, loaded(n + 1, 0))
                        round_x(there)
                        root(n + 1)
                if more:
                    round_ft(g + 1, parity)

            def image(n, final):
                here, there = act.snap(slot(n)), act.snap(slot(n + 1))
                step(n, 0, 1, here, there, first=True)
                with act.Fori(0, 2) as jj:
                    step(n, 2 * jj + 1, 0, here, there)
                    step(n, 2 * jj + 2, 1, here, there)
                step(n, 5, 0, here, there, norm=not final)
                step(n, 6, 0, here, there, last=True, more=not final)

            act.wait_ge(wnorm2_ready, 1)
            nc.scalar.activation(wnorm[:, :], wnorm2[:, :], ACT.Sqrt).then_inc(wnorm_ready, 1)
            act.wait_ge(first_loaded[0], 16)
            round_x(0)
            root(0)
            act.wait_ge(bias_ready, 1)
            make_f(0)
            act.wait_ge(first_loaded[1], 16)
            round_x(CHUNK)
            round_ft(0, 0)
            with act.Fori(0, N - 1) as n:
                image(n, False)
            image(N - 1, True)

        @block.vector
        def _(dve):
            links = [0]

            def link(ins):
                links[0] += 1
                ins.then_inc(dve_chain, 1)
                dve.wait_ge(dve_chain, links[0])

            nc.vector.memset(newton[:, :], 0.0).then_inc(y_added, Y_BANKS)

            dve.wait_ge(setup_mm, 1)
            link(nc.vector.tensor_copy(taps[:, :], small_bank[:, 0:KC]))
            s = 2 * T1 + 2 * T2
            for at, a0, b0, T, k in ((0, 0, T1, T1, s), (T1, 2 * T1, 2 * T1 + T2, T2, s + 2)):
                nc.vector.tensor_scalar(tap_coef[:, 1, at:at + T], taps[:, a0:a0 + T], taps[:, k:k + 1],
                                        None, ALU.mult)
                link(nc.vector.tensor_scalar(tap_coef[:, 0, at:at + T], taps[:, b0:b0 + T], taps[:, k:k + 1],
                                             taps[:, k + 1:k + 2], ALU.mult, ALU.add))

            link(nc.vector.tensor_tensor(wsq[:, :], wconv_raw[:, :], wconv_raw[:, :], ALU.mult))
            nc.vector.tensor_reduce(wnorm2[:, :], wsq[:, :].rearrange("p (g e) -> p g e", e=CPG),
                                    AX.X, ALU.add).then_inc(wnorm2_ready, 1)
            link(nc.vector.tensor_scalar(babs[:, :], bconv[:, :], -1.0, None, ALU.mult))
            link(nc.vector.tensor_tensor(babs[:, :], babs[:, :], bconv[:, :], ALU.max))
            dve.wait_ge(wnorm_ready, 1)
            link(nc.vector.tensor_reduce(wreach[:, :], wnorm[:, :], AX.X, ALU.add))
            link(nc.vector.tensor_scalar(bound[:, 0:1], wreach[:, :], XN_MEAN_MAX, babs[:, 0:1], ALU.mult, ALU.add))
            link(nc.vector.tensor_scalar(bound[:, 1:2], wreach[:, :], XN_MAX, babs[:, 0:1], ALU.mult, ALU.add))
            link(nc.vector.tensor_scalar(bound[:, 0:1], bound[:, 0:1], 1.0, None, ALU.max))
            link(nc.vector.tensor_scalar(bound[:, 2:3], bound[:, 1:2], bound[:, 0:1], TINY, ALU.mult, ALU.max))
            link(nc.vector.tensor_scalar(tap_abs[:, :, :], tap_coef[:, :, :], -1.0, None, ALU.mult))
            link(nc.vector.tensor_tensor(tap_abs[:, :, :], tap_abs[:, :, :], tap_coef[:, :, :], ALU.max))
            link(nc.vector.tensor_reduce(bound[:, 3:4], tap_abs[:, :, :].rearrange("p a t -> p (a t)"),
                                         AX.X, ALU.max))
            link(nc.vector.tensor_scalar(bound[:, 3:4], bound[:, 3:4], TINY, None, ALU.max))
            link(nc.vector.tensor_scalar(bound[:, 2:4].bitcast(U32), bound[:, 2:4].bitcast(U32), 0x7F800000,
                                         None, ALU.bitwise_and))
            link(nc.vector.reciprocal(bound[:, 0:2], bound[:, 2:4]))
            nc.vector.tensor_scalar(f_scale[:, :], bound[:, 0:1], TOP * SPLIT, None, ALU.mult)
            nc.vector.tensor_scalar(o_scale[:, :], bound[:, 2:3], 1.0 / TOP, bound[:, 3:4], ALU.mult, ALU.mult)
            link(nc.vector.tensor_scalar(tap_scale[:, :], bound[:, 1:2], TOP, None, ALU.mult))
            link(nc.vector.tensor_scalar(o_scale[:, :], o_scale[:, :], 1.0 / TOP, None, ALU.mult))
            link(nc.vector.tensor_scalar(tap_coef[:, :, :], tap_coef[:, :, :], tap_scale[:, 0:1], None, ALU.mult))

            dve.wait_ge(setup_mm, 2)
            nc.vector.tensor_copy(wconv_t[:, :, :],
                                  y_bank[0][:, :].rearrange("p (t o) -> p t o", t=CT)).then_inc(wconv_ready, 1)
            dve.wait_ge(setup_mm, 3)
            link(nc.vector.tensor_copy(wfuse_t[:, :, :], y_bank[1][:, 0:2 * P].rearrange("p (h o) -> p h o", h=2)))
            link(nc.vector.tensor_copy(wfuse_hi[:, :, :], wfuse_t[:, :, :]))
            nc.vector.tensor_tensor(wfuse_lo[:, :, :], wfuse_t[:, :, :], wfuse_hi[:, :, :].bitcast(F32),
                                    ALU.subtract).then_inc(wfuse_ready, 1)

            def channel_stats(at, k, tiles=range(CT)):
                for t in tiles:
                    ins = nc.vector.bn_stats(stats[:, t, bass.ds(BN * k, BN)], x_ring[:, t, bass.ds(at, CHUNK)])
                return ins

            def small(ins, n, k):
                ins.then_inc(norm_step, 1)
                dve.wait_ge(norm_step, NORM_STEPS * n + k)

            def norm_channels(n):
                dve.wait_ge(stats_done, 2 * n + 2)
                nc.vector.memset(newton[:, :], 0.0)
                for t in range(CT):
                    ins = nc.vector.bn_aggr(chan[:, t, :], stats[:, t, :])
                ins.then_inc(chan_ready, 1)

            def norm_deviations(n):
                dve.wait_ge(grp_done, 2 * n + 1)
                small(nc.vector.tensor_copy(grp[:, :, :], small_bank[:, 0:2 * CT].rearrange("p (t s) -> p t s", s=2)),
                      n, 1)
                small(nc.vector.tensor_tensor(dev[:, :], chan[:, :, 0], grp[:, :, 0], ALU.subtract), n, 2)
                nc.vector.tensor_tensor(dev2[:, :], dev[:, :], dev[:, :], ALU.mult).then_inc(dev_ready, 1)

            def norm_variance(n):
                dve.wait_ge(grp_done, 2 * n + 2)
                nc.vector.scalar_tensor_tensor(var[:, :], small_bank[:, VAR_AT:VAR_AT + CT], EPS, grp[:, :, 1],
                                               ALU.add, ALU.add).then_inc(var_ready, 1)

            def norm_factors(n):
                dve.wait_ge(std_ready, n + 1)
                small(nc.vector.reciprocal(rstd[:, :], std[:, :]), n, 3)
                small(nc.vector.tensor_tensor(newton[:, :], rstd[:, :], rstd[:, :], ALU.mult), n, 4)
                small(nc.vector.tensor_tensor(newton[:, :], newton[:, :], var[:, :], ALU.mult), n, 5)
                small(nc.vector.tensor_scalar(newton[:, :], newton[:, :], -0.5, 1.5, ALU.mult, ALU.add), n, 6)
                small(nc.vector.tensor_tensor(rvec[:, :], newton[:, :], rstd[:, :], ALU.mult), n, 7)
                nc.vector.scalar_tensor_tensor(shift_pair[:, :, 0], grp[:, :, 0], -1.0, rvec[:, :],
                                               ALU.mult, ALU.mult)
                nc.vector.tensor_tensor(shift_pair[:, :, 1], dev[:, :], rvec[:, :], ALU.mult).then_inc(pair_ready, 1)

            def norm_weights(n):
                for t in range(CT):
                    ins = nc.vector.tensor_scalar(wn[:, t, :], wconv_t[:, t, :], rvec[:, t:t + 1], None, ALU.mult)
                small(ins, n, 8)
                small(nc.vector.tensor_copy(wn_hi[:, :, :], wn[:, :, :]), n, 9)
                nc.vector.tensor_tensor(wn_lo[:, :, :], wn[:, :, :], wn_hi[:, :, :].bitcast(F32),
                                        ALU.subtract).then_inc(wn_ready, 1)

            def norm_biases(n):
                dve.wait_ge(pair_done, n + 1)
                small(nc.vector.tensor_scalar(bias_f[:, :], small_bank[:, PAIR_AT:PAIR_AT + 1], bconv[:, 0:1],
                                              f_scale[:, 0:1], ALU.add, ALU.mult), n, 10)
                small(nc.vector.tensor_scalar(gain[:, :], small_bank[:, PAIR_AT + 1:PAIR_AT + 2], bconv[:, 0:1],
                                              0.0, ALU.add, ALU.max), n, 11)
                nc.vector.tensor_tensor(gain_f[:, :], f_scale[:, :], gain[:, :], ALU.mult)
                nc.vector.tensor_tensor(bias_g[:, :], bias_f[:, :], gain[:, :], ALU.mult).then_inc(bias_ready, 1)

            for j in range(GROUPS):
                dve.wait_ge(first_loaded[j], 16)
                ins = channel_stats(j * CHUNK, j)
            ins.then_inc(stats_done, 2)
            norm_channels(0)
            norm_deviations(0)
            norm_variance(0)
            norm_factors(0)
            norm_weights(0)
            norm_biases(0)

            for k, (width, step_by, first_tap) in enumerate(((K1, 1, 0), (K2, 2, T1))):
                for tap in range(width * width):
                    dr, dc = step_by * (tap // width), step_by * (tap % width)
                    view = shifts[0:TILE, dr:dr + WIN_ROWS, dc:dc + WIN_COLS]
                    for ab in range(2):
                        acc = band_f32[0:TILE, ab, k, :].rearrange("p (r c) -> p r c", c=WIN_COLS)
                        coef = tap_coef[0:TILE, ab, first_tap + tap:first_tap + tap + 1]
                        if tap == 0:
                            ins = nc.vector.tensor_scalar(acc, view, coef, None, ALU.mult)
                        else:
                            ins = nc.vector.scalar_tensor_tensor(acc, view, coef, acc, ALU.mult, ALU.add)
                    link(ins)
            link(nc.vector.tensor_copy(band_hi[0:TILE, :, :, :], band_f32[0:TILE, :, :, :]))
            nc.vector.tensor_scalar(band_hi_down[0:TILE, :, :, :], band_hi[0:TILE, :, :, :], 1.0 / SPLIT,
                                    None, ALU.mult)
            nc.vector.tensor_tensor(band_lo[0:TILE, :, :, :], band_f32[0:TILE, :, :, :],
                                    band_hi[0:TILE, :, :, :], ALU.subtract).then_inc(bands_ready, 1)

            def rest_of_band(b, to, value):
                dve.wait_ge(oh_ready, value)
                nc.vector.scalar_tensor_tensor(o_lo[:, to, :, :], band_columns(b), o_scale[:, 0:1],
                                               o_hi[:, to, :, :].bitcast(F32),
                                               ALU.mult, ALU.subtract).then_inc(ol_ready, 1)

            def rest_of_ft(g, parity):
                for a in range(2):
                    dve.wait_ge(fth_ready, 2 * g + a + 1)
                    nc.vector.scalar_tensor_tensor(ft_lo[0:TILE, parity, a, :], ft_hi[0:TILE, parity, a, :], -SPLIT,
                                                   ft_bank[a][0:TILE, :], ALU.mult, ALU.add).then_inc(ftl_ready, 1)

            def add_y(n, j, tiles, at):
                for t in tiles:
                    dve.wait_ge(y_done, y_no(n, j, t))
                    xs = x_ring[:, t, bass.ds(at, CHUNK)]
                    nc.vector.scalar_tensor_tensor(xs, y_bank[t % Y_BANKS][:, 0:CHUNK], bfuse[:, t % 2:t % 2 + 1],
                                                   xs, ALU.add, ALU.add).then_inc(y_added, 1)

            def add_y_band(done, at):
                for h in range(2):
                    dve.wait_ge(y_done, done[h])
                    xs = x_ring[:, h:h + 3:2, bass.ds(at, BAND)]
                    nc.vector.scalar_tensor_tensor(xs, band_columns(y_bank[h]), bfuse[:, h:h + 1],
                                                   xs, ALU.add, ALU.add).then_inc(y_added, 1)

            def next_stats(n, there, k, tiles=range(CT)):
                dve.wait_ge(x_loaded, loaded(n + 1, k))
                return channel_stats(there + k * CHUNK, k, tiles)

            def image(n, final):
                here, there = dve.snap(slot(n)), dve.snap(slot(n + 1))
                rest_of_band(even_bank, EVEN, even_split(n, 0))
                if not final:
                    next_stats(n, there, 0)
                rest_of_ft(group_no(n, 1), 1)
                add_y_band((y_first(n, 0), y_first(n, 1)), here)
                with dve.Fori(0, 2) as jj:
                    for odd in (1, 0):
                        j = 2 * jj + (1 if odd else 2)
                        at = here + j * CHUNK - BAND
                        rest_of_band(odd_bank, ODD, odd_split(n, j - 1))
                        rest_of_band(even_bank, EVEN, even_split(n, j))
                        if not final:
                            next_stats(n, there, 3 * jj + (1 if odd else 3))
                        add_y(n, j, (0, 1), at)
                        rest_of_ft(group_no(n, j) + 1, 1 - odd)
                        add_y(n, j, (2, 3), at)
                        if not final:
                            ins = next_stats(n, there, 3 * jj + 2, (0, 1) if odd else (2, 3))
                            if not odd:
                                ins.then_inc(stats_done, 1)
                if not final:
                    norm_channels(n + 1)
                rest_of_band(odd_bank, ODD, odd_split(n, 4))
                rest_of_band(even_bank, EVEN, even_split(n, 5))
                if not final:
                    norm_deviations(n + 1)
                    norm_variance(n + 1)
                add_y(n, 5, (0, 1), here + 5 * CHUNK - BAND)
                if not final:
                    norm_factors(n + 1)
                rest_of_ft(group_no(n, 6), 0)
                add_y(n, 5, (2, 3), here + 5 * CHUNK - BAND)
                if not final:
                    norm_weights(n + 1)
                rest_of_band(odd_bank, ODD, odd_split(n, 5))
                if not final:
                    norm_biases(n + 1)
                rest_of_band(even_bank, EVEN, even_split(n, 6))
                rest_of_band(odd_bank, TAIL, odd_split(n, 6))
                add_y(n, 6, range(CT), here + 6 * CHUNK - BAND)
                if not final:
                    rest_of_ft(group_no(n + 1, 0), 0)
                add_y_band((y_no(n, GROUPS, 0), y_no(n, GROUPS, 1)), here + HW - BAND)

            rest_of_ft(0, 0)
            with dve.Fori(0, N - 1) as n:
                image(n, False)
            image(N - 1, True)

        @block.tensor
        def _(pe):
            def three(dst, w, m, start, stop):
                nc.tensor.matmul(dst, w[0], m[0], start=start, stop=False)
                nc.tensor.matmul(dst, w[0], m[1], start=False, stop=False)
                return nc.tensor.matmul(dst, w[1], m[0], start=False, stop=stop)

            pe.wait_ge(params_loaded, 16 * 13)
            pe.wait_ge(masks_ready, 4)
            nc.tensor.matmul(small_bank[:, 0:KC], ones[:, :], taps_row[:, :], start=True, stop=True)\
                .then_inc(setup_mm, 1)
            for t in range(CT):
                ins = nc.tensor.transpose(y_bank[0][:, t * CM:(t + 1) * CM], wconv_raw[:, t * P:(t + 1) * P],
                                          ident[:, :])
            ins.then_inc(setup_mm, 1)
            for h in range(2):
                ins = nc.tensor.transpose(y_bank[1][:, h * P:(h + 1) * P], wfuse_raw[:, h, :], ident[:, :])
            ins.then_inc(setup_mm, 1)

            def average_channels(n):
                pe.wait_ge(chan_ready, n + 1)
                nc.tensor.matmul(small_bank[:, 0:2 * CT], group_avg[:, :], chan[:, :, :],
                                 start=True, stop=True).then_inc(grp_done, 1)

            def average_deviations(n):
                pe.wait_ge(dev_ready, n + 1)
                nc.tensor.matmul(small_bank[:, VAR_AT:VAR_AT + CT], group_avg[:, :], dev2[:, :],
                                 start=True, stop=True).then_inc(grp_done, 1)

            def conv_of_pair(n):
                pe.wait_ge(pair_ready, n + 1)
                for t in range(CT):
                    ins = nc.tensor.matmul(small_bank[:, PAIR_AT:PAIR_AT + 2], wconv_t[:, t, :], shift_pair[:, t, :],
                                           start=t == 0, stop=t == CT - 1)
                ins.then_inc(pair_done, 1)

            def conv_in(g):
                if not isinstance(g, int) or g > 0:
                    pe.wait_ge(f_ready, 2 * g)
                for t in range(CT):
                    pe.wait_ge(xl_ready, CT * g + t + 1)
                    ins = three(f_bank[:, 0:CHUNK], (wn_hi[:, t, :], wn_lo[:, t, :]),
                                (x_hi[:, t, :], x_lo[:, t, :]), t == 0, t == CT - 1)
                ins.then_inc(f_done, 1)

            def transposes(g):
                for a in range(2):
                    pe.wait_ge(f_ready, 2 * g + a + 1)
                    for q in range(COL_BLOCKS):
                        for b in range(ROW_BLOCKS):
                            t = ROW_BLOCKS * q + b
                            ins = nc.tensor.transpose(ft_bank[a][0:TILE, t * CM:(t + 1) * CM],
                                                      f_row[:, a, q, b * TILE:(b + 1) * TILE], ident[:, :])
                    ins.then_inc(t_done, 1)

            def bands(view, band_row, parity, fresh):
                pieces = [(a, q, b) for a in range(2) for q in range(COL_BLOCKS) for b in range(ROW_BLOCKS)
                          if share(b, band_row)[2] > 0]
                for a, q, b in pieces:
                    to_row, win_row, rows = share(b, band_row)
                    lo, hi, c0, c1 = window(q)
                    t = ROW_BLOCKS * q + b
                    dst = view[:, :, to_row:to_row + rows, lo:hi]
                    fh, fl = [v[0:TILE, parity, a, t * CM:(t + 1) * CM] for v in (ft_hi, ft_lo)]
                    bh, bl, bh_down = [v[0:TILE, a, :, :].rearrange("p k (r c) -> p k r c", c=WIN_COLS)
                                       [:, :, win_row:win_row + rows, c0:c1] for v in (band_hi, band_lo, band_hi_down)]
                    first, last = fresh and (a, q, b) == pieces[0], (a, q, b) == pieces[-1]
                    nc.tensor.matmul(dst, fh, bh, start=first, stop=False, skip_group_check=True)
                    nc.tensor.matmul(dst, fh, bl, start=False, stop=False, skip_group_check=True)
                    ins = nc.tensor.matmul(dst, fl, bh_down, start=False, stop=last, skip_group_check=True)
                return ins

            def fuse(n, j, tiles):
                for t in tiles:
                    pe.wait_ge(y_added, y_no(n, j, t))
                    h = t % 2
                    m = [o[:, ODD:EVEN + 1, t // 2, :] for o in (o_hi, o_lo)]
                    three(y_bank[t % Y_BANKS][:, 0:CHUNK], (wfuse_hi[:, h, :], wfuse_lo[:, h, :]), m,
                          True, True).then_inc(y_done, 1)

            def fuse_band(free, slot):
                for h in range(2):
                    pe.wait_ge(y_added, free[h])
                    m = [o[:, slot, :, :] for o in (o_hi, o_lo)]
                    three(y_bank[h][:, 0:CHUNK], (wfuse_hi[:, h, :], wfuse_lo[:, h, :]), m,
                          True, True).then_inc(y_done, 1)

            def step(n, j, parity, first=False, last=False, norm=False, more=True):
                g = group_no(n, j)
                pe.wait_ge(ftl_ready, 2 * g + 2)
                if not first:
                    bands(odd_v, -BAND_ROWS, parity, False).then_inc(odd_done, 1)
                bands(even_v, 0, parity, first).then_inc(even_done, 1)
                if norm:
                    average_channels(n + 1)
                if more:
                    if last:
                        pe.wait_ge(wn_ready, n + 2)
                    conv_in(g + 1)
                if norm:
                    average_deviations(n + 1)
                if not first:
                    pe.wait_ge(ol_ready, odd_split(n, j - 1))
                ins = bands(odd_v, BAND_ROWS, parity, True)
                if last:
                    ins.then_inc(odd_done, 1)
                pe.wait_ge(ol_ready, even_split(n, j))
                if not first:
                    fuse(n, j, range(CT) if last else (0, 1))
                if more:
                    transposes(g + 1)
                if not last:
                    bands(even_v, 2 * BAND_ROWS, parity, True)
                if first:
                    fuse_band((y_first(n, 0), y_first(n, 1)), EVEN)
                elif last:
                    pe.wait_ge(ol_ready, odd_split(n, j))
                    fuse_band((y_no(n, GROUPS, 0), y_no(n, GROUPS, 1)), TAIL)
                else:
                    fuse(n, j, (2, 3))
                if norm:
                    conv_of_pair(n + 1)

            def image(n, final):
                step(n, 0, 0, first=True)
                with pe.Fori(0, 2) as jj:
                    step(n, 2 * jj + 1, 1)
                    step(n, 2 * jj + 2, 0)
                step(n, 5, 1, norm=not final)
                step(n, 6, 0, last=True, more=not final)

            average_channels(0)
            average_deviations(0)
            conv_of_pair(0)
            pe.wait_ge(wn_ready, 1)
            conv_in(0)
            transposes(0)
            pe.wait_ge(wfuse_ready, 1)
            pe.wait_ge(bands_ready, 1)
            with pe.Fori(0, N - 1) as n:
                image(n, False)
            image(N - 1, True)


_INS = ["x"] + ["L0_conv_" + k for k in
                ("W_conv", "b_conv", "wk", "bk", "wck", "bck", "wk2", "bk2", "wck2", "bck2", "W_fuse", "b_fuse")]


def kernel(**inputs):
    import numpy as _np
    import concourse.bacc as _bacc
    from concourse import mybir as _mybir
    from concourse.bass_utils import run_bass_kernel_spmd as _run

    nc = _bacc.Bacc("TRN2", target_bir_lowering=False, num_devices=1)
    arrays, args = {}, []
    for name in _INS:
        a = _np.ascontiguousarray(inputs[name])
        a = a.reshape(a.shape or (1,))
        arrays[f"in_{name}_dram"] = a
        args.append(nc.dram_tensor(f"in_{name}_dram", a.shape, _mybir.dt.from_np(a.dtype), kind="ExternalInput").ap())
    shape = tuple(inputs["x"].shape)
    args.append(nc.dram_tensor("out_0_dram", shape, _mybir.dt.float32, kind="ExternalOutput").ap())
    build(nc, *args)
    r = _run(nc, [arrays], core_ids=[0])
    return r.results[0]["out_0_dram"]
```

```python
from contextlib import ExitStack

import concourse.bass as bass
from concourse import mybir

ALU = mybir.AluOpType
ACT = mybir.ActivationFunctionType
AX = mybir.AxisListType
F32 = mybir.dt.float32
F32R = mybir.dt.float32r
F16 = mybir.dt.float16
U32 = mybir.dt.uint32

P = 128
N, C, H, W = 32, 512, 56, 56
CM = 128
CT = C // P
CPG = 16
EPS = 1e-5
K1, K2 = 5, 3
HALO = 2
HW = H * W

GROUP_ROWS = 8
GROUPS = H // GROUP_ROWS
CHUNK = GROUP_ROWS * W
BAND_ROWS = GROUP_ROWS // 2
BAND = BAND_ROWS * W
TILE_ROWS, TILE_COLS = 8, 14
TILE = TILE_ROWS * TILE_COLS
ROW_BLOCKS = GROUP_ROWS // TILE_ROWS
COL_BLOCKS = W // TILE_COLS
TILES = ROW_BLOCKS * COL_BLOCKS
WIN_ROWS = TILE_ROWS + 2 * HALO
WIN_COLS = TILE_COLS + 2 * HALO
WIN = WIN_ROWS * WIN_COLS

RING = 2 * GROUPS
AHEAD = RING - 1
CHUNKS = N * GROUPS

Y_BANK = (0, 1, 2, 0)
Y_START = 1
BN = 6
VAR_AT, GAIN_AT = 2 * CT, P
NORM_STEPS = 11
EVEN, ODD = range(2)
SEAM = HALO * W

SPLIT = 2.0 ** 11
TOP = 2.0 ** 14
XN_MAX = (CPG * HW) ** 0.5
XN_MEAN_MAX = CPG ** 0.5
TINY = 2.0 ** -60


def window(q):
    left, right = TILE_COLS * q - HALO, TILE_COLS * (q + 1) + HALO
    lo, hi = max(left, 0), min(right, W)
    return lo, hi, lo - left, hi - left


def share(b, band_row, top, bottom):
    reach = TILE_ROWS * b - HALO
    lo = max(reach, band_row, top)
    hi = min(reach + WIN_ROWS, band_row + BAND_ROWS, bottom)
    return lo - band_row, lo - reach, hi - lo


def build(nc, x, w_conv, b_conv, wk, bk, wck, bck, wk2, bk2, wck2, bck2, w_fuse, b_fuse, out):
    x_chunks = x.rearrange("n (t p) h w -> n p t (h w)", p=P)
    out_chunks = out.rearrange("n (t p) h w -> n p t (h w)", p=P)

    with ExitStack() as ctx:
        def sb(name, shape, dt=F32):
            return ctx.enter_context(nc.sbuf_tensor(name, shape, dt))

        def bank(name):
            return ctx.enter_context(nc.psum_tensor(name, [P, 512], F32))

        def sem(name):
            return ctx.enter_context(nc.semaphore(name))

        x_ring = sb("x_ring", [P, CT, RING * CHUNK])
        x_hi = sb("x_hi", [P, CT, CHUNK + 2], F32R)
        x_lo = sb("x_lo", [P, CT, CHUNK + 2], F32R)
        f_row = sb("f_row", [P, COL_BLOCKS, ROW_BLOCKS * TILE])
        gft = sb("gft", [P, TILES * CM])
        gain_rows = sb("gain_rows", [P, CM])
        ft_hi = sb("ft_hi", [P, 3, 2, TILES * CM], F16)
        ft_lo = sb("ft_lo", [P, 3, 2, TILES * CM], F16)
        o_hi = sb("o_hi", [P, 2, 2, BAND], F32R)
        o_lo = sb("o_lo", [P, 2, 2, BAND], F32R)
        band_hi = sb("band_hi", [P, 2, 2, WIN], F16)
        band_lo = sb("band_lo", [P, 2, 2, WIN], F16)
        band_hi_down = sb("band_hi_down", [P, 2, 2, WIN], F16)
        band_f32 = sb("band_f32", [P, 2, 2, WIN])
        place = sb("place", [P, TILE_ROWS, WIN_COLS + 2 * HALO])
        row_place = sb("row_place", [P, TILE_ROWS])
        col_place = sb("col_place", [P, WIN_COLS + 2 * HALO])
        tap_rows = [sb("tap_rows1", [P, 2, K1, K1]), sb("tap_rows2", [P, 2, K2, K2])]
        lines = [sb("lines1", [P, 2, K1, WIN_COLS]), sb("lines2", [P, 2, K2, WIN_COLS])]
        band_term = sb("band_term", [P, 2, K1, WIN_COLS])
        wconv_raw = sb("wconv_raw", [P, C])
        wfuse_raw = sb("wfuse_raw", [P, 2, CM])
        wconv_t = sb("wconv_t", [P, CT, CM])
        wn = sb("wn", [P, CT, CM])
        wn_hi = sb("wn_hi", [P, CT, CM], F32R)
        wn_lo = sb("wn_lo", [P, CT, CM], F32R)
        wfuse_t = sb("wfuse_t", [P, 2, P])
        wfuse_hi = sb("wfuse_hi", [P, 2, P], F32R)
        wfuse_lo = sb("wfuse_lo", [P, 2, P], F32R)
        ident = sb("ident", [P, P])
        group_avg = sb("group_avg", [P, P])
        ones = sb("ones", [P, P])
        T1, T2 = K1 * K1, K2 * K2
        KC = 2 * T1 + 2 * T2 + 4
        taps_row = sb("taps_row", [1, KC])
        taps = sb("taps", [P, KC])
        tap_coef = sb("tap_coef", [P, 2, T1 + T2])
        bconv = sb("bconv", [P, 1])
        bfuse = sb("bfuse", [P, 2])
        stats = sb("stats", [P, CT, GROUPS * BN])
        chan = sb("chan", [P, CT, 2])
        grp = sb("grp", [P, CT, 2])
        dev = sb("dev", [P, CT])
        dev2 = sb("dev2", [P, CT])
        var = sb("var", [P, CT])
        std = sb("std", [P, CT])
        rstd = sb("rstd", [P, CT])
        newton = sb("newton", [P, CT])
        rvec = sb("rvec", [P, CT])
        shift_pair = sb("shift_pair", [P, CT, 2])
        wsq = sb("wsq", [P, C])
        wnorm2 = sb("wnorm2", [P, C // CPG])
        wnorm = sb("wnorm", [P, C // CPG])
        wreach = sb("wreach", [P, 1])
        babs = sb("babs", [P, 1])
        bound = sb("bound", [P, 4])
        tap_abs = sb("tap_abs", [P, 2, T1 + T2])
        f_scale = sb("f_scale", [P, 1])
        tap_scale = sb("tap_scale", [P, 1])
        o_scale = sb("o_scale", [P, 1])
        bias_f = sb("bias_f", [P, 1])
        gain = sb("gain", [P, 1])

        odd_bank = bank("odd_bank")
        even_bank = bank("even_bank")
        f_bank = bank("f_bank")
        ft_bank = bank("ft_bank")
        y_bank = [bank("y_bank0"), bank("y_bank1"), bank("y_bank2")]
        small_bank = bank("small_bank")

        def band_view(b):
            return b[:, 0:2 * BAND].rearrange("p (k r w) -> p k r w", k=2, w=W)

        odd_v, even_v = band_view(odd_bank), band_view(even_bank)

        def band_columns(b):
            return b[:, 0:2 * BAND].rearrange("p (k n) -> p k n", k=2)

        first_loaded = [sem(f"first_loaded{k}") for k in range(GROUPS)]
        x_loaded = sem("x_loaded")
        y_stored = sem("y_stored")
        params_loaded = sem("params_loaded")
        seam_zeroed = sem("seam_zeroed")
        masks_zeroed = sem("masks_zeroed")
        masks_ready = sem("masks_ready")
        setup_mm = sem("setup_mm")
        wconv_ready = sem("wconv_ready")
        wfuse_ready = sem("wfuse_ready")
        wnorm2_ready = sem("wnorm2_ready")
        wnorm_ready = sem("wnorm_ready")
        bands_ready = sem("bands_ready")
        dve_chain = sem("dve_chain")
        norm_step = sem("norm_step")
        stats_done = sem("stats_done")
        chan_ready = sem("chan_ready")
        grp_done = sem("grp_done")
        dev_ready = sem("dev_ready")
        var_ready = sem("var_ready")
        std_ready = sem("std_ready")
        pair_ready = sem("pair_ready")
        wn_ready = sem("wn_ready")
        gain_ready = sem("gain_ready")
        gain_done = sem("gain_done")
        gain_rows_ready = sem("gain_rows_ready")
        coef_ready = sem("coef_ready")
        bands_zeroed = sem("bands_zeroed")
        places_ready = sem("places_ready")
        bands_step = sem("bands_step")
        lines_ready = sem("lines_ready")
        bands2_ready = sem("bands2_ready")
        xh_ready = sem("xh_ready")
        xl_ready = sem("xl_ready")
        f_done = sem("f_done")
        f_ready = sem("f_ready")
        t_done = sem("t_done")
        gft_ready = sem("gft_ready")
        fth_ready = sem("fth_ready")
        ftl_ready = sem("ftl_ready")
        odd_done = sem("odd_done")
        even_done = sem("even_done")
        oh_ready = sem("oh_ready")
        ol_ready = sem("ol_ready")
        y_done = sem("y_done")
        y_added = sem("y_added")

        block = ctx.enter_context(nc.Block())

        def slot(n):
            return (n % 2) * HW

        def ft_slot(j):
            return 2 if j == GROUPS - 1 else j % 2

        def group_no(n, j):
            return GROUPS * n + j

        def even_split(g):
            return 2 * g + 1

        def odd_split(g):
            return 2 * g + 2

        def y_no(g, t):
            return CT * g + t + 1

        def loaded(n, j):
            return 16 * (group_no(n, j) - GROUPS + 1)

        @block.sync
        def _(sp):
            def load(n, j, signal):
                at = (GROUPS * n + j) * CHUNK
                sp.dma_start(x_ring[:, :, at:at + CHUNK],
                             x_chunks[n, :, :, j * CHUNK:(j + 1) * CHUNK]).then_inc(signal, 16)

            load(0, 0, first_loaded[0])
            sp.dma_start(wconv_raw[:, :], w_conv).then_inc(params_loaded, 16)
            sp.dma_start(wfuse_raw[:, :, :], w_fuse.rearrange("(h p) c -> p h c", p=P)).then_inc(params_loaded, 16)
            sp.dma_start(bconv[:, :], b_conv.rearrange("(p a) -> p a", a=1)).then_inc(params_loaded, 16)
            for h in range(2):
                sp.dma_start(bfuse[:, h:h + 1], b_fuse[h * P:(h + 1) * P].rearrange("(p a) -> p a", a=1))\
                    .then_inc(params_loaded, 16)
            at = 0
            for v, size in ((wk, T1), (bk, T1), (wk2, T2), (bk2, T2), (wck, 1), (bck, 1), (wck2, 1), (bck2, 1)):
                sp.dma_start(taps_row[:, at:at + size], v.rearrange("(a n) -> a n", a=1)).then_inc(params_loaded, 16)
                at += size
            for k in range(1, GROUPS):
                load(0, k, first_loaded[k])
            for k in range(GROUPS, AHEAD):
                load(1, k - GROUPS, x_loaded)
                sp.wait_ge(x_loaded, loaded(1, k - GROUPS))

            START = 16 * (AHEAD - GROUPS)
            sp.sem_inc(y_stored, START)

            def store(k, earlier=True):
                n, j = k // GROUPS, k % GROUPS
                if isinstance(k, int) and k == CHUNKS - 1:
                    sp.wait_ge(y_added, Y_START + CT * CHUNKS + CT // 2)
                else:
                    sp.wait_ge(y_added, Y_START + y_no(k + 1, CT - 1))
                if earlier:
                    sp.wait_ge(y_stored, 16 * k + START)
                    sp.wait_ge(x_loaded, 16 * k + START if loads else START + 16 * (CHUNKS - AHEAD))
                sp.dma_start(out_chunks[n, :, :, bass.ds(j * CHUNK, CHUNK)],
                             x_ring[:, :, bass.ds((k % RING) * CHUNK, CHUNK)]).then_inc(y_stored, 16)

            def load_ahead(k):
                m = k + AHEAD
                sp.dma_start(x_ring[:, :, bass.ds((m % RING) * CHUNK, CHUNK)],
                             x_chunks[m // GROUPS, :, :, bass.ds(m % GROUPS * CHUNK, CHUNK)]).then_inc(x_loaded, 16)

            loads = True
            store(0, earlier=False)
            load_ahead(0)
            with sp.Fori(1, CHUNKS - AHEAD) as k:
                store(k)
                load_ahead(k)
            loads = False
            with sp.Fori(CHUNKS - AHEAD, CHUNKS - 1) as k:
                store(k)
            store(CHUNKS - 1)
            sp.wait_ge(y_stored, START + 16 * CHUNKS)

        @block.gpsimd
        def _(pool):
            pool.memset(ident[:, :], 0.0).then_inc(masks_zeroed, 1)
            pool.memset(place[:, :, :], 0.0).then_inc(masks_zeroed, 1)
            pool.memset(group_avg[:, :], 1.0 / CPG).then_inc(masks_zeroed, 1)
            pool.memset(x_ring[:, :, 2 * HW - SEAM:2 * HW], 0.0).then_inc(seam_zeroed, 1)
            pool.memset(ones[:, :], 1.0).then_inc(masks_ready, 1)
            pool.memset(band_f32[:, :, :, :], 0.0).then_inc(bands_zeroed, 1)
            pool.wait_ge(masks_zeroed, 3)
            pool.affine_select(out=ident[:, :], in_=ident[:, :], compare_op=ALU.not_equal, fill=1.0,
                               base=0, pattern=[[-1, P]], channel_multiplier=1).then_inc(masks_ready, 1)
            inner = place[0:TILE, :, 2 * HALO:2 * HALO + TILE_COLS]
            pool.affine_select(out=inner, in_=inner, compare_op=ALU.not_equal, fill=1.0, base=0,
                               pattern=[[TILE_COLS, TILE_ROWS], [1, TILE_COLS]],
                               channel_multiplier=-1).then_inc(masks_ready, 1)
            ga = group_avg[:, :].rearrange("p (g e) -> p g e", e=CPG)
            pool.affine_select(out=ga, in_=ga, compare_op=ALU.is_ge, fill=0.0, base=0,
                               pattern=[[-CPG, P // CPG], [0, CPG]], channel_multiplier=1).then_inc(masks_zeroed, 1)
            pool.wait_ge(masks_zeroed, 4)
            pool.affine_select(out=ga, in_=ga, compare_op=ALU.is_ge, fill=0.0, base=CPG - 1,
                               pattern=[[CPG, P // CPG], [0, CPG]], channel_multiplier=-1).then_inc(masks_ready, 1)

            def split_x(n, j, at):
                for t in range(CT):
                    pool.wait_ge(xh_ready, CT * group_no(n, j) + t + 1)
                    pool.tensor_tensor(x_lo[:, t, 0:CHUNK], x_ring[:, t, bass.ds(at, CHUNK)],
                                       x_hi[:, t, 0:CHUNK].bitcast(F32), ALU.subtract).then_inc(xl_ready, 1)

            def image(n, final):
                here, there = pool.snap(slot(n)), pool.snap(slot(n + 1))
                split_x(n, 2, here + 2 * CHUNK)
                with pool.Fori(0, 4) as jj:
                    split_x(n, jj + 3, here + (jj + 3) * CHUNK)
                if not final:
                    split_x(n + 1, 0, there)
                    split_x(n + 1, 1, there + CHUNK)

            split_x(0, 0, 0)

            steps = [0]

            def link(ins):
                steps[0] += 1
                ins.then_inc(bands_step, 1)
                pool.wait_ge(bands_step, steps[0])

            pool.wait_ge(places_ready, 2)
            pool.wait_ge(coef_ready, 1)
            for k, width, dilation in ((0, K1, 1), (1, K2, 2)):
                for c in range(width):
                    coef = tap_rows[k][0:TILE, :, :, c:c + 1].broadcast_to([TILE, 2, width, WIN_COLS])
                    at = col_place[0:TILE, dilation * c:dilation * c + WIN_COLS]\
                        .rearrange("p (a b c) -> p a b c", a=1, b=1).broadcast_to([TILE, 2, width, WIN_COLS])
                    to = lines[k] if c == 0 else band_term
                    link(pool.tensor_tensor(to[0:TILE, :, 0:width, :], coef, at, ALU.mult))
                    if c > 0:
                        acc = lines[k][0:TILE, :, :, :]
                        link(pool.tensor_tensor(acc, acc, band_term[0:TILE, :, 0:width, :], ALU.add))
                if k == 0:
                    pool.sem_inc(lines_ready, 1)
            pool.wait_ge(bands_zeroed, 1)
            rows2 = band_f32[0:TILE, :, 1, :].rearrange("p a (r c) -> p a r c", c=WIN_COLS)
            for row in range(TILE_ROWS):
                term, acc = band_term[0:TILE, :, 0:K2, :], rows2[:, :, row:row + 2 * K2 - 1:2, :]
                link(pool.tensor_scalar(term, lines[1][0:TILE, :, :, :], row_place[0:TILE, row:row + 1],
                                        None, ALU.mult))
                link(pool.tensor_tensor(acc, acc, term, ALU.add))
            pool.sem_inc(bands2_ready, 1)

            split_x(0, 1, CHUNK)
            with pool.Fori(0, N - 1) as n:
                image(n, False)
            image(N - 1, True)

        @block.scalar
        def _(act):
            def root(n):
                act.wait_ge(var_ready, n + 1)
                nc.scalar.activation(std[:, :], var[:, :], ACT.Sqrt).then_inc(std_ready, 1)

            def round_x(at, tiles):
                for t in tiles:
                    nc.scalar.activation(x_hi[:, t, 0:CHUNK], x_ring[:, t, bass.ds(at, CHUNK)],
                                         ACT.Copy).then_inc(xh_ready, 1)

            def make_f(g):
                act.wait_ge(f_done, g + 1)
                by_rows = f_bank[:, 0:CHUNK].rearrange("p (r q c) -> p r q c", q=COL_BLOCKS, c=TILE_COLS)
                by_tiles = f_row[:, :, :].rearrange("p q (r c) -> p r q c", c=TILE_COLS)
                nc.scalar.activation(by_tiles, by_rows, ACT.Relu,
                                     bias=bias_f[:, 0:1], scale=f_scale[:, 0:1]).then_inc(f_ready, 1)

            def round_ft(g, to):
                act.wait_ge(t_done, g + 1)
                nc.scalar.activation(ft_hi[0:TILE, to, 0, :], ft_bank[0:TILE, :],
                                     ACT.Copy, scale=1.0 / SPLIT).then_inc(fth_ready, 1)

            def round_gft(g, to):
                act.wait_ge(gft_ready, g + 1)
                nc.scalar.activation(ft_hi[0:TILE, to, 1, :], gft[0:TILE, :],
                                     ACT.Copy, scale=1.0 / SPLIT).then_inc(fth_ready, 1)

            def round_band(b, to):
                nc.scalar.activation(o_hi[:, :, to, :], band_columns(b), ACT.Copy,
                                     scale=o_scale[:, 0:1]).then_inc(oh_ready, 1)

            def step(n, j, like, here, there, final=False):
                g = group_no(n, j)
                last, norm = like == GROUPS - 1, like == GROUPS - 2
                to = ft_slot((like + 1) % GROUPS)
                act.wait_ge(even_done, g + 1)
                round_band(even_bank, EVEN)
                act.wait_ge(odd_done, g + 1)
                round_band(odd_bank, ODD)
                if last and final:
                    act.wait_ge(even_done, CHUNKS + 1)
                    nc.scalar.activation(o_hi[:, :, EVEN, 0:SEAM], band_columns(even_bank)[:, :, 0:SEAM],
                                         ACT.Copy, scale=o_scale[:, 0:1]).then_inc(oh_ready, 1)
                    return
                if last:
                    act.wait_ge(gain_ready, n + 2)
                make_f(g + 1)
                if norm and not final:
                    root(n + 1)
                rounds = not (norm and final)
                if last or (norm and rounds):
                    act.wait_ge(x_loaded, loaded(n + 1, 1 if last else 0))
                    ahead = there + (CHUNK if last else 0)
                else:
                    ahead = here + (j + 2) * CHUNK
                early = (0,) if last else (0, 1)
                if rounds:
                    round_x(ahead, early)
                round_ft(g + 1, to)
                if rounds:
                    round_x(ahead, range(len(early), CT - 1))
                round_gft(g + 1, to)
                if rounds:
                    round_x(ahead, (3,))

            def image(n, final):
                here, there = act.snap(slot(n)), act.snap(slot(n + 1))
                step(n, 0, 0, here, there)
                with act.Fori(0, 2) as jj:
                    step(n, 2 * jj + 1, 1, here, there)
                    step(n, 2 * jj + 2, 2, here, there)
                step(n, 5, 5, here, there, final)
                step(n, 6, 6, here, there, final)

            act.wait_ge(wnorm2_ready, 1)
            nc.scalar.activation(wnorm[:, :], wnorm2[:, :], ACT.Sqrt).then_inc(wnorm_ready, 1)
            act.wait_ge(first_loaded[0], 16)
            round_x(0, range(CT))
            root(0)
            act.wait_ge(gain_ready, 1)
            make_f(0)
            act.wait_ge(first_loaded[1], 16)
            round_x(CHUNK, range(CT))
            round_ft(0, 0)
            round_gft(0, 0)
            with act.Fori(0, N - 1) as n:
                image(n, False)
            image(N - 1, True)

        @block.vector
        def _(dve):
            links = [0]

            def link(ins):
                links[0] += 1
                ins.then_inc(dve_chain, 1)
                dve.wait_ge(dve_chain, links[0])

            nc.vector.memset(newton[:, :], 0.0).then_inc(y_added, Y_START)
            nc.vector.memset(even_bank[:, :], 0.0).then_inc(seam_zeroed, 1)

            dve.wait_ge(masks_ready, 3)
            nc.vector.tensor_reduce(row_place[0:TILE, :], place[0:TILE, :, :], AX.X, ALU.add).then_inc(places_ready, 1)
            nc.vector.tensor_reduce(col_place[0:TILE, :], place[0:TILE, :, :].rearrange("p r c -> p c r"),
                                    AX.X, ALU.add).then_inc(places_ready, 1)

            def channel_stats(at, k, tiles=range(CT)):
                for t in tiles:
                    ins = nc.vector.bn_stats(stats[:, t, bass.ds(BN * k, BN)], x_ring[:, t, bass.ds(at, CHUNK)])
                return ins

            dve.wait_ge(first_loaded[0], 16)
            channel_stats(0, 0)

            dve.wait_ge(setup_mm, 1)
            link(nc.vector.tensor_copy(taps[:, :], small_bank[:, 0:KC]))
            s = 2 * T1 + 2 * T2
            for at, a0, b0, T, k in ((0, 0, T1, T1, s), (T1, 2 * T1, 2 * T1 + T2, T2, s + 2)):
                nc.vector.tensor_scalar(tap_coef[:, 1, at:at + T], taps[:, a0:a0 + T], taps[:, k:k + 1],
                                        None, ALU.mult)
                link(nc.vector.tensor_scalar(tap_coef[:, 0, at:at + T], taps[:, b0:b0 + T], taps[:, k:k + 1],
                                             taps[:, k + 1:k + 2], ALU.mult, ALU.add))

            link(nc.vector.tensor_tensor(wsq[:, :], wconv_raw[:, :], wconv_raw[:, :], ALU.mult))
            nc.vector.tensor_reduce(wnorm2[:, :], wsq[:, :].rearrange("p (g e) -> p g e", e=CPG),
                                    AX.X, ALU.add).then_inc(wnorm2_ready, 1)
            link(nc.vector.tensor_scalar(babs[:, :], bconv[:, :], -1.0, None, ALU.mult))
            link(nc.vector.tensor_tensor(babs[:, :], babs[:, :], bconv[:, :], ALU.max))
            dve.wait_ge(wnorm_ready, 1)
            link(nc.vector.tensor_reduce(wreach[:, :], wnorm[:, :], AX.X, ALU.add))
            link(nc.vector.tensor_scalar(bound[:, 0:1], wreach[:, :], XN_MEAN_MAX, babs[:, 0:1], ALU.mult, ALU.add))
            link(nc.vector.tensor_scalar(bound[:, 1:2], wreach[:, :], XN_MAX, babs[:, 0:1], ALU.mult, ALU.add))
            link(nc.vector.tensor_scalar(bound[:, 0:1], bound[:, 0:1], 1.0, None, ALU.max))
            link(nc.vector.tensor_scalar(bound[:, 2:3], bound[:, 1:2], bound[:, 0:1], TINY, ALU.mult, ALU.max))
            link(nc.vector.tensor_scalar(tap_abs[:, :, :], tap_coef[:, :, :], -1.0, None, ALU.mult))
            link(nc.vector.tensor_tensor(tap_abs[:, :, :], tap_abs[:, :, :], tap_coef[:, :, :], ALU.max))
            link(nc.vector.tensor_reduce(bound[:, 3:4], tap_abs[:, :, :].rearrange("p a t -> p (a t)"),
                                         AX.X, ALU.max))
            link(nc.vector.tensor_scalar(bound[:, 3:4], bound[:, 3:4], TINY, None, ALU.max))
            link(nc.vector.tensor_scalar(bound[:, 2:4].bitcast(U32), bound[:, 2:4].bitcast(U32), 0x7F800000,
                                         None, ALU.bitwise_and))
            link(nc.vector.reciprocal(bound[:, 0:2], bound[:, 2:4]))
            nc.vector.tensor_scalar(f_scale[:, :], bound[:, 0:1], TOP * SPLIT, None, ALU.mult)
            nc.vector.tensor_scalar(o_scale[:, :], bound[:, 2:3], 1.0 / TOP, bound[:, 3:4], ALU.mult, ALU.mult)
            link(nc.vector.tensor_scalar(tap_scale[:, :], bound[:, 1:2], TOP, None, ALU.mult))
            link(nc.vector.tensor_scalar(o_scale[:, :], o_scale[:, :], 1.0 / TOP, None, ALU.mult))
            for k, width in enumerate((K1, K2)):
                for row in range(width):
                    at = k * T1 + row * width
                    ins = nc.vector.tensor_scalar(tap_rows[k][:, :, width - 1 - row, :], tap_coef[:, :, at:at + width],
                                                  tap_scale[:, 0:1], None, ALU.mult)
            ins.then_inc(coef_ready, 1)

            dve.wait_ge(setup_mm, 2)
            nc.vector.tensor_copy(wconv_t[:, :, :],
                                  y_bank[0][:, :].rearrange("p (t o) -> p t o", t=CT)).then_inc(wconv_ready, 1)
            dve.wait_ge(setup_mm, 3)
            link(nc.vector.tensor_copy(wfuse_t[:, :, :], y_bank[1][:, 0:2 * P].rearrange("p (h o) -> p h o", h=2)))
            link(nc.vector.tensor_copy(wfuse_hi[:, :, :], wfuse_t[:, :, :]))
            nc.vector.tensor_tensor(wfuse_lo[:, :, :], wfuse_t[:, :, :], wfuse_hi[:, :, :].bitcast(F32),
                                    ALU.subtract).then_inc(wfuse_ready, 1)

            def small(ins, n, k):
                ins.then_inc(norm_step, 1)
                dve.wait_ge(norm_step, NORM_STEPS * n + k)

            def norm_channels(n):
                dve.wait_ge(stats_done, 2 * n + 2)
                nc.vector.memset(newton[:, :], 0.0)
                for t in range(CT):
                    ins = nc.vector.bn_aggr(chan[:, t, :], stats[:, t, :])
                ins.then_inc(chan_ready, 1)

            def norm_deviations(n):
                dve.wait_ge(grp_done, 2 * n + 1)
                small(nc.vector.tensor_copy(grp[:, :, :], small_bank[:, 0:2 * CT].rearrange("p (t s) -> p t s", s=2)),
                      n, 1)
                small(nc.vector.tensor_tensor(dev[:, :], chan[:, :, 0], grp[:, :, 0], ALU.subtract), n, 2)
                nc.vector.tensor_tensor(dev2[:, :], dev[:, :], dev[:, :], ALU.mult).then_inc(dev_ready, 1)
                nc.vector.tensor_scalar(shift_pair[:, :, 0], grp[:, :, 0], -1.0, None, ALU.mult)
                small(nc.vector.tensor_copy(shift_pair[:, :, 1], dev[:, :]), n, 3)
                pair_hi, pair_lo = x_hi[:, :, CHUNK:CHUNK + 2], x_lo[:, :, CHUNK:CHUNK + 2]
                small(nc.vector.tensor_copy(pair_hi, shift_pair[:, :, :]), n, 4)
                nc.vector.tensor_tensor(pair_lo, shift_pair[:, :, :], pair_hi.bitcast(F32),
                                        ALU.subtract).then_inc(pair_ready, 1)

            def norm_variance(n):
                dve.wait_ge(grp_done, 2 * n + 2)
                nc.vector.scalar_tensor_tensor(var[:, :], small_bank[:, VAR_AT:VAR_AT + CT], EPS, grp[:, :, 1],
                                               ALU.add, ALU.add).then_inc(var_ready, 1)

            def norm_factors(n):
                dve.wait_ge(std_ready, n + 1)
                small(nc.vector.reciprocal(rstd[:, :], std[:, :]), n, 5)
                small(nc.vector.tensor_tensor(newton[:, :], rstd[:, :], rstd[:, :], ALU.mult), n, 6)
                small(nc.vector.tensor_tensor(newton[:, :], newton[:, :], var[:, :], ALU.mult), n, 7)
                small(nc.vector.tensor_scalar(newton[:, :], newton[:, :], -0.5, 1.5, ALU.mult, ALU.add), n, 8)
                small(nc.vector.tensor_tensor(rvec[:, :], newton[:, :], rstd[:, :], ALU.mult), n, 9)

            def norm_weights(n):
                for t in range(CT):
                    ins = nc.vector.tensor_scalar(wn[:, t, :], wconv_t[:, t, :], rvec[:, t:t + 1], None, ALU.mult)
                ins.then_inc(norm_step, 1)

            def split_weights(n):
                dve.wait_ge(norm_step, NORM_STEPS * n + 10)
                small(nc.vector.tensor_copy(wn_hi[:, :, :], wn[:, :, :]), n, 11)
                nc.vector.tensor_tensor(wn_lo[:, :, :], wn[:, :, :], wn_hi[:, :, :].bitcast(F32),
                                        ALU.subtract).then_inc(wn_ready, 1)

            def norm_biases(n):
                dve.wait_ge(f_done, group_no(n, 0) + 1)
                pair = f_bank[:, CHUNK:CHUNK + 2]
                nc.vector.tensor_scalar(bias_f[:, :], pair[:, 0:1], bconv[:, 0:1],
                                        f_scale[:, 0:1], ALU.add, ALU.mult)
                nc.vector.tensor_scalar(gain[:, :], pair[:, 1:2], bconv[:, 0:1],
                                        0.0, ALU.add, ALU.max).then_inc(gain_ready, 1)

            def norm_gain(n):
                dve.wait_ge(gain_done, n + 1)
                nc.vector.tensor_copy(gain_rows[:, :], small_bank[:, GAIN_AT:GAIN_AT + CM]).then_inc(gain_rows_ready, 1)
                dve.wait_ge(gain_rows_ready, n + 1)

            for j in range(1, GROUPS):
                dve.wait_ge(first_loaded[j], 16)
                ins = channel_stats(j * CHUNK, j)
            ins.then_inc(stats_done, 2)
            norm_channels(0)
            norm_deviations(0)
            norm_variance(0)
            norm_factors(0)
            norm_weights(0)
            split_weights(0)

            dve.wait_ge(lines_ready, 1)
            dve.wait_ge(bands_zeroed, 1)
            rows1 = band_f32[0:TILE, :, 0, :].rearrange("p a (r c) -> p a r c", c=WIN_COLS)
            for row in range(TILE_ROWS):
                acc = rows1[:, :, row:row + K1, :]
                link(nc.vector.scalar_tensor_tensor(acc, lines[0][0:TILE, :, :, :], row_place[0:TILE, row:row + 1],
                                                    acc, ALU.mult, ALU.add))
            dve.wait_ge(bands2_ready, 1)
            link(nc.vector.tensor_copy(band_hi[0:TILE, :, :, :], band_f32[0:TILE, :, :, :]))
            nc.vector.tensor_scalar(band_hi_down[0:TILE, :, :, :], band_hi[0:TILE, :, :, :], 1.0 / SPLIT,
                                    None, ALU.mult)
            nc.vector.tensor_tensor(band_lo[0:TILE, :, :, :], band_f32[0:TILE, :, :, :],
                                    band_hi[0:TILE, :, :, :], ALU.subtract).then_inc(bands_ready, 1)
            norm_biases(0)
            norm_gain(0)

            def rest_of_band(b, to, value):
                dve.wait_ge(oh_ready, value)
                nc.vector.scalar_tensor_tensor(o_lo[:, :, to, :], band_columns(b), o_scale[:, 0:1],
                                               o_hi[:, :, to, :].bitcast(F32),
                                               ALU.mult, ALU.subtract).then_inc(ol_ready, 1)

            def rest_of_ft(g, to):
                dve.wait_ge(fth_ready, 2 * g + 1)
                nc.vector.scalar_tensor_tensor(ft_lo[0:TILE, to, 0, :], ft_hi[0:TILE, to, 0, :], -SPLIT,
                                               ft_bank[0:TILE, :], ALU.mult, ALU.add).then_inc(ftl_ready, 1)

            def make_gft(g):
                dve.wait_ge(fth_ready, 2 * g + 1)
                gains = gain_rows[0:TILE, :].rearrange("p (a c) -> p a c", a=1).broadcast_to([TILE, TILES, CM])
                nc.vector.tensor_tensor(gft[0:TILE, :].rearrange("p (t c) -> p t c", c=CM),
                                        ft_bank[0:TILE, :].rearrange("p (t c) -> p t c", c=CM), gains,
                                        ALU.mult).then_inc(gft_ready, 1)

            def rest_of_gft(g, to):
                dve.wait_ge(fth_ready, 2 * g + 2)
                nc.vector.scalar_tensor_tensor(ft_lo[0:TILE, to, 1, :], ft_hi[0:TILE, to, 1, :], -SPLIT,
                                               gft[0:TILE, :], ALU.mult, ALU.add).then_inc(ftl_ready, 1)

            def add_y(g, tiles, at, before=None):
                for t in tiles:
                    dve.wait_ge(y_done, y_no(g, t))
                    parts = ([(before, 0, SEAM), (at, SEAM, CHUNK)] if before is not None
                             else [(at, 0, CHUNK)])
                    for start, lo, hi in parts:
                        xs = x_ring[:, t, bass.ds(start, hi - lo)]
                        ins = nc.vector.scalar_tensor_tensor(xs, y_bank[Y_BANK[t]][:, lo:hi],
                                                             bfuse[:, t % 2:t % 2 + 1], xs, ALU.add, ALU.add)
                    ins.then_inc(y_added, 1)

            def next_stats(n, there, k, tiles=range(CT)):
                dve.wait_ge(x_loaded, loaded(n + 1, k))
                return channel_stats(there + k * CHUNK, k, tiles)

            def image(n, final):
                here, there = dve.snap(slot(n)), dve.snap(slot(n + 1))
                g = group_no(n, 0)
                rest_of_band(even_bank, EVEN, even_split(g))
                rest_of_band(odd_bank, ODD, odd_split(g))
                if not final:
                    next_stats(n, there, 0)
                add_y(g, (0, 1), here, there + HW - SEAM)
                rest_of_ft(g + 1, ft_slot(1))
                make_gft(g + 1)
                add_y(g, (2,), here, there + HW - SEAM)
                rest_of_gft(g + 1, ft_slot(1))
                add_y(g, (3,), here, there + HW - SEAM)
                with dve.Fori(0, 2) as jj:
                    for like in (1, 2):
                        j = 2 * jj + like
                        g = group_no(n, j)
                        at = here + j * CHUNK - SEAM
                        if not final:
                            ins = next_stats(n, there, 3 * jj + 2, (0, 1) if like == 1 else (2, 3))
                            if like == 2:
                                ins.then_inc(stats_done, 1)
                        rest_of_band(even_bank, EVEN, even_split(g))
                        rest_of_band(odd_bank, ODD, odd_split(g))
                        if not final:
                            ins = next_stats(n, there, 3 * jj + (1 if like == 1 else 3))
                            if like == 2:
                                ins.then_inc(stats_done, 1)
                        add_y(g, (0, 1), at)
                        rest_of_ft(g + 1, ft_slot(like + 1))
                        make_gft(g + 1)
                        add_y(g, (2,), at)
                        rest_of_gft(g + 1, ft_slot(like + 1))
                        add_y(g, (3,), at)
                g, at = group_no(n, 5), here + 5 * CHUNK - SEAM
                if not final:
                    norm_channels(n + 1)
                rest_of_band(even_bank, EVEN, even_split(g))
                rest_of_band(odd_bank, ODD, odd_split(g))
                if not final:
                    norm_deviations(n + 1)
                    norm_variance(n + 1)
                add_y(g, (0,), at)
                if not final:
                    norm_factors(n + 1)
                rest_of_ft(g + 1, ft_slot(6))
                make_gft(g + 1)
                if not final:
                    norm_weights(n + 1)
                rest_of_gft(g + 1, ft_slot(6))
                if not final:
                    split_weights(n + 1)
                add_y(g, (1, 2, 3), at)
                g, at = group_no(n, 6), here + 6 * CHUNK - SEAM
                rest_of_band(even_bank, EVEN, even_split(g))
                rest_of_band(odd_bank, ODD, odd_split(g))
                if not final:
                    norm_biases(n + 1)
                add_y(g, (0, 1), at)
                if not final:
                    norm_gain(n + 1)
                    make_gft(g + 1)
                    rest_of_ft(g + 1, ft_slot(0))
                    rest_of_gft(g + 1, ft_slot(0))
                add_y(g, (2, 3), at)
                if final:
                    dve.wait_ge(oh_ready, even_split(CHUNKS))
                    nc.vector.scalar_tensor_tensor(o_lo[:, :, EVEN, 0:SEAM], band_columns(even_bank)[:, :, 0:SEAM],
                                                   o_scale[:, 0:1], o_hi[:, :, EVEN, 0:SEAM].bitcast(F32),
                                                   ALU.mult, ALU.subtract).then_inc(ol_ready, 1)
                    for h in range(2):
                        dve.wait_ge(y_done, y_no(CHUNKS, h))
                        xs = x_ring[:, h:h + 3:2, bass.ds(here + HW - SEAM, SEAM)]
                        nc.vector.scalar_tensor_tensor(
                            xs, y_bank[h][:, 0:2 * SEAM].rearrange("p (k n) -> p k n", k=2), bfuse[:, h:h + 1],
                            xs, ALU.add, ALU.add).then_inc(y_added, 1)

            rest_of_ft(0, 0)
            make_gft(0)
            rest_of_gft(0, 0)
            with dve.Fori(0, N - 1) as n:
                image(n, False)
            image(N - 1, True)

        @block.tensor
        def _(pe):
            def three(dst, w, m, start, stop):
                nc.tensor.matmul(dst, w[0], m[0], start=start, stop=False)
                nc.tensor.matmul(dst, w[0], m[1], start=False, stop=False)
                return nc.tensor.matmul(dst, w[1], m[0], start=False, stop=stop)

            pe.wait_ge(params_loaded, 16 * 13)
            pe.wait_ge(masks_ready, 4)
            nc.tensor.matmul(small_bank[:, 0:KC], ones[0:1, :], taps_row[:, :], start=True, stop=True)\
                .then_inc(setup_mm, 1)
            for t in range(CT):
                ins = nc.tensor.transpose(y_bank[0][:, t * CM:(t + 1) * CM], wconv_raw[:, t * P:(t + 1) * P],
                                          ident[:, :])
            ins.then_inc(setup_mm, 1)
            for h in range(2):
                ins = nc.tensor.transpose(y_bank[1][:, h * P:(h + 1) * P], wfuse_raw[:, h, :], ident[:, :])
            ins.then_inc(setup_mm, 1)

            def average_channels(n):
                pe.wait_ge(chan_ready, n + 1)
                nc.tensor.matmul(small_bank[:, 0:2 * CT], group_avg[:, :], chan[:, :, :],
                                 start=True, stop=True).then_inc(grp_done, 1)

            def average_deviations(n):
                pe.wait_ge(dev_ready, n + 1)
                nc.tensor.matmul(small_bank[:, VAR_AT:VAR_AT + CT], group_avg[:, :], dev2[:, :],
                                 start=True, stop=True).then_inc(grp_done, 1)

            def spread_gain(n):
                pe.wait_ge(gain_ready, n + 1)
                nc.tensor.transpose(small_bank[:, GAIN_AT:GAIN_AT + CM], gain[:, 0:1].broadcast_to([P, CM]),
                                    ident[:, :]).then_inc(gain_done, 1)

            def conv_in(g, n=None):
                width = CHUNK
                if n is not None:
                    width = CHUNK + 2
                    pe.wait_ge(pair_ready, n + 1)
                if not isinstance(g, int) or g > 0:
                    pe.wait_ge(f_ready, g)
                for t in range(CT):
                    pe.wait_ge(xl_ready, CT * g + t + 1)
                    if n is not None and t == 0:
                        pe.wait_ge(wn_ready, n + 1)
                    ins = three(f_bank[:, 0:width], (wn_hi[:, t, :], wn_lo[:, t, :]),
                                (x_hi[:, t, 0:width], x_lo[:, t, 0:width]), t == 0, t == CT - 1)
                ins.then_inc(f_done, 1)

            def transposes(g):
                pe.wait_ge(f_ready, g + 1)
                for q in range(COL_BLOCKS):
                    for b in range(ROW_BLOCKS):
                        t = ROW_BLOCKS * q + b
                        ins = nc.tensor.transpose(ft_bank[0:TILE, t * CM:(t + 1) * CM],
                                                  f_row[:, q, b * TILE:(b + 1) * TILE], ident[:, :])
                ins.then_inc(t_done, 1)

            def bands(view, band_row, like, factors=(0, 1), fresh=False):
                top = 0 if like == 0 else -HALO
                bottom = GROUP_ROWS if like == GROUPS - 1 else GROUP_ROWS + HALO
                pieces = [(a, q, b) for a in factors for q in range(COL_BLOCKS) for b in range(ROW_BLOCKS)
                          if share(b, band_row, top, bottom)[2] > 0]
                for a, q, b in pieces:
                    to_row, win_row, rows = share(b, band_row, top, bottom)
                    lo, hi, c0, c1 = window(q)
                    t = ROW_BLOCKS * q + b
                    dst = view[:, :, to_row:to_row + rows, lo:hi]
                    fh, fl = [v[0:TILE, ft_slot(like), a, t * CM:(t + 1) * CM] for v in (ft_hi, ft_lo)]
                    bh, bl, bh_down = [v[0:TILE, a, :, :].rearrange("p k (r c) -> p k r c", c=WIN_COLS)
                                       [:, :, win_row:win_row + rows, c0:c1] for v in (band_hi, band_lo, band_hi_down)]
                    first, last = fresh and (a, q, b) == pieces[0], (a, q, b) == pieces[-1]
                    nc.tensor.matmul(dst, fh, bh, start=first, stop=False, skip_group_check=True)
                    nc.tensor.matmul(dst, fh, bl, start=False, stop=False, skip_group_check=True)
                    ins = nc.tensor.matmul(dst, fl, bh_down, start=False, stop=last, skip_group_check=True)
                return ins

            def fuse(g, tiles):
                for t in tiles:
                    if t == 0:
                        pe.wait_ge(y_added, Y_START + y_no(g, 0) - 1)
                    elif t == 3:
                        pe.wait_ge(y_added, Y_START + y_no(g, 0))
                    h = t % 2
                    m = [o[:, t // 2, :, :].rearrange("p s n -> p (s n)") for o in (o_hi, o_lo)]
                    three(y_bank[Y_BANK[t]][:, 0:CHUNK], (wfuse_hi[:, h, :], wfuse_lo[:, h, :]), m,
                          True, True).then_inc(y_done, 1)

            def step(n, j, like, final=False):
                g = group_no(n, j)
                last, norm = like == GROUPS - 1, like == GROUPS - 2 and not final
                more = not (last and final)
                pe.wait_ge(ftl_ready, 2 * g + 1)
                bands(even_v, -HALO, like, (0,))
                bands(odd_v, BAND_ROWS - HALO, like, (0,), fresh=True)
                pe.wait_ge(ftl_ready, 2 * g + 2)
                bands(even_v, -HALO, like, (1,)).then_inc(even_done, 1)
                bands(odd_v, BAND_ROWS - HALO, like, (1,)).then_inc(odd_done, 1)
                if norm:
                    average_channels(n + 1)
                if more:
                    conv_in(g + 1, n + 1 if last else None)
                if norm:
                    average_deviations(n + 1)
                pe.wait_ge(ol_ready, odd_split(g))
                fuse(g, (0, 1) if more else range(CT))
                if more:
                    if last:
                        spread_gain(n + 1)
                    transposes(g + 1)
                ins = bands(even_v, 2 * BAND_ROWS - HALO, like, fresh=True)
                if more:
                    fuse(g, (2, 3))
                    return
                ins.then_inc(even_done, 1)
                pe.wait_ge(ol_ready, even_split(CHUNKS))
                for h in range(2):
                    pe.wait_ge(y_added, Y_START + y_no(CHUNKS - 1, CT - 1))
                    m = [o[:, :, EVEN, 0:SEAM] for o in (o_hi, o_lo)]
                    three(y_bank[h][:, 0:2 * SEAM], (wfuse_hi[:, h, :], wfuse_lo[:, h, :]), m,
                          True, True).then_inc(y_done, 1)

            def image(n, final):
                step(n, 0, 0)
                with pe.Fori(0, 2) as jj:
                    step(n, 2 * jj + 1, 1)
                    step(n, 2 * jj + 2, 2)
                step(n, 5, 5, final)
                step(n, 6, 6, final)

            average_channels(0)
            average_deviations(0)
            conv_in(0, 0)
            spread_gain(0)
            transposes(0)
            pe.wait_ge(wfuse_ready, 1)
            pe.wait_ge(bands_ready, 1)
            pe.wait_ge(seam_zeroed, 2)
            with pe.Fori(0, N - 1) as n:
                image(n, False)
            image(N - 1, True)


_INS = ["x"] + ["L0_conv_" + k for k in
                ("W_conv", "b_conv", "wk", "bk", "wck", "bck", "wk2", "bk2", "wck2", "bck2", "W_fuse", "b_fuse")]


def kernel(**inputs):
    import numpy as _np
    import concourse.bacc as _bacc
    from concourse import mybir as _mybir
    from concourse.bass_utils import run_bass_kernel_spmd as _run

    nc = _bacc.Bacc("TRN2", target_bir_lowering=False, num_devices=1)
    arrays, args = {}, []
    for name in _INS:
        a = _np.ascontiguousarray(inputs[name])
        a = a.reshape(a.shape or (1,))
        arrays[f"in_{name}_dram"] = a
        args.append(nc.dram_tensor(f"in_{name}_dram", a.shape, _mybir.dt.from_np(a.dtype), kind="ExternalInput").ap())
    shape = tuple(inputs["x"].shape)
    args.append(nc.dram_tensor("out_0_dram", shape, _mybir.dt.float32, kind="ExternalOutput").ap())
    build(nc, *args)
    r = _run(nc, [arrays], core_ids=[0])
    return r.results[0]["out_0_dram"]
```
